# Optimizing a Trainium2 kernel written in Bass

```python
import numpy as np
import jax
import jax.numpy as jnp

def _softmax(x, axis=-1):
    return jax.nn.softmax(x, axis=axis)
def _gelu(x):
    return jax.nn.gelu(x, approximate=True)
def _silu(x):
    return jax.nn.silu(x)
def _sigmoid(x):
    return jax.nn.sigmoid(x)
def _layernorm(x, axis=-1, eps=1e-5):
    m = jnp.mean(x, axis=axis, keepdims=True)
    v = jnp.var(x, axis=axis, keepdims=True)
    return (x - m) / jnp.sqrt(v + eps)
def _scatter_add(tgt, idx, src, axis=0):
    return tgt.at[idx].add(src)
def _segment_sum(src, seg, n):
    return jax.ops.segment_sum(src, seg, n)

kernel_name = 'mk_conv_seq_d2_conv_nchw256_01032a'

def setup_inputs(seed: int = 0):
    np.random.seed(seed)
    _w = jnp.asarray
    def _rec_inputs():
        import jax
        import jax.numpy as jnp
        _gk = jax.random.key(seed)
        x = -0.0005207 + 1.001 * jax.random.normal(jax.random.fold_in(_gk, 1), (2, 256, 64, 64), jnp.float32)
        return x
    x = _rec_inputs()
    def _L0_conv_setup():
        import jax, jax.numpy as jnp
        import numpy as np
        GROUPS = 32
        NUM_HEADS = 4
        EPS = 1e-05

        def group_norm(x, weight, bias):
            b, c, h, w = x.shape
            xg = x.reshape(b, GROUPS, c // GROUPS, h, w)
            mu = xg.mean(axis=(2, 3, 4), keepdims=True)
            var = xg.var(axis=(2, 3, 4), keepdims=True)
            xn = ((xg - mu) * jax.lax.rsqrt(var + EPS)).reshape(b, c, h, w)
            return xn * weight[None, :, None, None] + bias[None, :, None, None]
        key = jax.random.key(seed)
        ks = jax.random.split(key, 5)
        B, C, H, W = (2, 256, 64, 64)
        x = jax.random.normal(ks[0], (B, C, H, W), dtype=jnp.float32)
        gn_weight = jnp.ones((C,), dtype=jnp.float32)
        gn_bias = jnp.zeros((C,), dtype=jnp.float32)
        qkv_weight = jax.random.normal(ks[1], (3 * C, C), dtype=jnp.float32) / np.sqrt(C)
        qkv_bias = jax.random.normal(ks[2], (3 * C,), dtype=jnp.float32) * 0.02
        proj_weight = jax.random.normal(ks[3], (C, C), dtype=jnp.float32) / np.sqrt(C)
        proj_bias = jax.random.normal(ks[4], (C,), dtype=jnp.float32) * 0.02
        return {'x': x, 'gn_weight': gn_weight, 'gn_bias': gn_bias, 'qkv_weight': qkv_weight, 'qkv_bias': qkv_bias, 'proj_weight': proj_weight, 'proj_bias': proj_bias}
    _L0_conv_all = _L0_conv_setup()
    _L0_conv_in = {k: v for k, v in _L0_conv_all.items() if k in ('gn_weight', 'gn_bias', 'qkv_weight', 'qkv_bias', 'proj_weight', 'proj_bias', )}
    del _L0_conv_all

    def _L1_conv_setup():
        import jax, jax.numpy as jnp
        import numpy as np
        EPS = 1e-05

        def batch_norm(x, gamma, beta):
            mean = jnp.mean(x, axis=(0, 2, 3), keepdims=True)
            var = jnp.mean((x - mean) ** 2, axis=(0, 2, 3), keepdims=True)
            xhat = (x - mean) * jax.lax.rsqrt(var + EPS)
            return xhat * gamma[None, :, None, None] + beta[None, :, None, None]

        def quantize_w1bit(w):
            E = jax.lax.stop_gradient(jnp.mean(jnp.abs(w)))
            wq = E * jnp.sign(w)
            return w + jax.lax.stop_gradient(wq - w)

        def conv3x3(x, w):
            return jax.lax.conv_general_dilated(x, w, window_strides=(1, 1), padding=((1, 1), (1, 1)), dimension_numbers=('NCHW', 'OIHW', 'NCHW'))
        key = jax.random.key(seed)
        ks = jax.random.split(key, 3)
        B, Cin, Cout, H, W = (32, 256, 256, 56, 56)
        return {'x': jax.random.normal(ks[0], (B, Cin, H, W), jnp.float32), 'gamma0': jnp.ones((Cin,), jnp.float32), 'beta0': jnp.zeros((Cin,), jnp.float32), 'w0': jax.random.normal(ks[1], (Cout, Cin, 3, 3), jnp.float32) * 0.05, 'gamma1': jnp.ones((Cout,), jnp.float32), 'beta1': jnp.zeros((Cout,), jnp.float32), 'w1': jax.random.normal(ks[2], (Cout, Cout, 3, 3), jnp.float32) * 0.05}
    _L1_conv_all = _L1_conv_setup()
    _L1_conv_in = {k: v for k, v in _L1_conv_all.items() if k in ('gamma0', 'beta0', 'w0', 'gamma1', 'beta1', 'w1', )}
    del _L1_conv_all

    return {
        "x": x,
        "L0_conv_gn_weight": _L0_conv_in["gn_weight"],
        "L0_conv_gn_bias": _L0_conv_in["gn_bias"],
        "L0_conv_qkv_weight": _L0_conv_in["qkv_weight"],
        "L0_conv_qkv_bias": _L0_conv_in["qkv_bias"],
        "L0_conv_proj_weight": _L0_conv_in["proj_weight"],
        "L0_conv_proj_bias": _L0_conv_in["proj_bias"],
        "L1_conv_gamma0": _L1_conv_in["gamma0"],
        "L1_conv_beta0": _L1_conv_in["beta0"],
        "L1_conv_w0": _L1_conv_in["w0"],
        "L1_conv_gamma1": _L1_conv_in["gamma1"],
        "L1_conv_beta1": _L1_conv_in["beta1"],
        "L1_conv_w1": _L1_conv_in["w1"],
    }

def reference(x, L0_conv_gn_weight, L0_conv_gn_bias, L0_conv_qkv_weight, L0_conv_qkv_bias, L0_conv_proj_weight, L0_conv_proj_bias, L1_conv_gamma0, L1_conv_beta0, L1_conv_w0, L1_conv_gamma1, L1_conv_beta1, L1_conv_w1):
    import jax
    import jax.numpy as jnp
    def _L0_conv_ref(x, gn_weight, gn_bias, qkv_weight, qkv_bias, proj_weight, proj_bias):
        import jax, jax.numpy as jnp
        import numpy as np
        GROUPS = 32
        NUM_HEADS = 4
        EPS = 1e-05

        def group_norm(x, weight, bias):
            b, c, h, w = x.shape
            xg = x.reshape(b, GROUPS, c // GROUPS, h, w)
            mu = xg.mean(axis=(2, 3, 4), keepdims=True)
            var = xg.var(axis=(2, 3, 4), keepdims=True)
            xn = ((xg - mu) * jax.lax.rsqrt(var + EPS)).reshape(b, c, h, w)
            return xn * weight[None, :, None, None] + bias[None, :, None, None]
        b, c, h, w = x.shape
        nh = NUM_HEADS
        hd = c // nh
        x_in = x
        xn = group_norm(x, gn_weight, gn_bias)
        qkv = jnp.einsum('oc,bchw->bohw', qkv_weight, xn) + qkv_bias[None, :, None, None]
        q, k, v = jnp.split(qkv, 3, axis=1)
        q = q.reshape(b, nh, hd, h * w)
        k = k.reshape(b, nh, hd, h * w)
        v = v.reshape(b, nh, hd, h * w)
        attn = jnp.einsum('bhdk,bhdq->bhkq', q, k) / np.sqrt(hd).astype(np.float32)
        attn = jax.nn.softmax(attn, axis=-1)
        out = jnp.einsum('bhkq,bhdq->bhdk', attn, v).reshape(b, c, h, w)
        out = jnp.einsum('oc,bchw->bohw', proj_weight, out) + proj_bias[None, :, None, None]
        return x_in + out

    def _L1_conv_ref(x, gamma0, beta0, w0, gamma1, beta1, w1):
        import jax, jax.numpy as jnp
        import numpy as np
        EPS = 1e-05

        def batch_norm(x, gamma, beta):
            mean = jnp.mean(x, axis=(0, 2, 3), keepdims=True)
            var = jnp.mean((x - mean) ** 2, axis=(0, 2, 3), keepdims=True)
            xhat = (x - mean) * jax.lax.rsqrt(var + EPS)
            return xhat * gamma[None, :, None, None] + beta[None, :, None, None]

        def quantize_w1bit(w):
            E = jax.lax.stop_gradient(jnp.mean(jnp.abs(w)))
            wq = E * jnp.sign(w)
            return w + jax.lax.stop_gradient(wq - w)

        def conv3x3(x, w):
            return jax.lax.conv_general_dilated(x, w, window_strides=(1, 1), padding=((1, 1), (1, 1)), dimension_numbers=('NCHW', 'OIHW', 'NCHW'))
        out = jax.nn.relu(batch_norm(x, gamma0, beta0))
        shortcut = x
        out = conv3x3(out, quantize_w1bit(w0))
        out = jax.nn.relu(batch_norm(out, gamma1, beta1))
        out = conv3x3(out, quantize_w1bit(w1))
        return out + shortcut

    def _gn(v, G=32, eps=1e-5):
        B_, C_, H_, W_ = v.shape
        g = v.reshape(B_, G, C_ // G, H_, W_)
        m = jnp.mean(g, axis=(2, 3, 4), keepdims=True)
        s = jnp.var(g, axis=(2, 3, 4), keepdims=True)
        return ((g - m) / jnp.sqrt(s + eps)).reshape(v.shape)

    def _ln_c(v, eps=1e-6):
        m = jnp.mean(v, axis=1, keepdims=True)
        s = jnp.var(v, axis=1, keepdims=True)
        return (v - m) / jnp.sqrt(s + eps)

    def _ln_t(v, eps=1e-5):
        m = jnp.mean(v, axis=-1, keepdims=True)
        s = jnp.var(v, axis=-1, keepdims=True)
        return (v - m) / jnp.sqrt(s + eps)

    def _to_tokens(v):
        B_, C_, H_, W_ = v.shape
        return v.reshape(B_, C_, H_ * W_).transpose(0, 2, 1)
    def _from_tokens(t, like):
        B_, C_, H_, W_ = like.shape
        return t.transpose(0, 2, 1).reshape(B_, C_, H_, W_)

    x = _L0_conv_ref(x, L0_conv_gn_weight, L0_conv_gn_bias, L0_conv_qkv_weight, L0_conv_qkv_bias, L0_conv_proj_weight, L0_conv_proj_bias)
    x = _L1_conv_ref(x, L1_conv_gamma0, L1_conv_beta0, L1_conv_w0, L1_conv_gamma1, L1_conv_beta1, L1_conv_w1)
    return x


_drawn_inputs = setup_inputs


def setup_inputs(seed=0):
    import zlib

    import numpy as np

    out = dict(_drawn_inputs(seed))
    spreads = {'L0_conv_gn_weight': (1.0, 0.2),
     'L0_conv_gn_bias': (0.0, 0.1),
     'L1_conv_gamma0': (1.0, 0.2),
     'L1_conv_beta0': (0.0, 0.1),
     'L1_conv_gamma1': (1.0, 0.2),
     'L1_conv_beta1': (0.0, 0.1)}
    factors = {'L0_conv_qkv_bias': 4.161, 'L0_conv_proj_bias': 5.059}
    for name, (base, spread) in spreads.items():
        noise = np.random.default_rng([zlib.crc32(name.encode()), seed]).standard_normal(out[name].shape)
        drawn = base * np.exp(spread * noise) if base else spread * noise
        out[name] = jnp.asarray(drawn.astype(out[name].dtype))
    for name, factor in factors.items():
        out[name] = (out[name] * factor).astype(out[name].dtype)
    return out
```

```python
from contextlib import ExitStack

import numpy as np

import concourse.bass as bass
from concourse import mybir

ALU = mybir.AluOpType
ACT = mybir.ActivationFunctionType
F32 = mybir.dt.float32
F16 = mybir.dt.float16
AX = mybir.AxisListType
RMAX = bass.bass_isa.ReduceOp.max

P = 128
B, C, H, W = 2, 256, 64, 64
CB = C // P
HEADS = 4
HD = C // HEADS
GROUPS = 32
N = H * W
TB = 512
NB = N // TB
KT = N // P
QT = TB // P
UNITS = 2 * QT * NB
PBUF = 4
TAPS = 9
PW = W + 2
ROWS = TB // W
EPS = 1e-5
GN_EPS = BN_EPS = EPS
SHIFT = 32768.0
RANGE = 4096.0
GN_MAX = float(np.sqrt(C // GROUPS * N))
BN_MAX = float(np.sqrt(B * N))

GW, GB, QKVB, PB, BN0, BN1 = 0, 2, 4, 10, 12, 16
NPAR = 20
IDENT, GAVG, MASK = 0, P, 2 * P
NCONST = 2 * P + TB


def units_of(kt):
    first = 3 * kt if kt < 8 else 24 + 2 * (kt - 8)
    return range(min(first, UNITS), min(first + (3 if kt < 8 else 2), UNITS))


class Shared:
    pass


def build(nc, x, qkv_t, proj_t, w0_t, w1_t, par_d, const_d, out):
    x1_d = nc.dram_tensor("x1_scratch", (B, CB, P, N), F32, kind="Internal").ap()
    with ExitStack() as top:
        def sem(name):
            return top.enter_context(nc.semaphore(name))

        def sb(stack, name, shape, dt=F32):
            return stack.enter_context(nc.sbuf_tensor(name, shape, dt))

        ps = top.enter_context(nc.psum_tensor("ps", [P, 8, TB], F32))
        ps_s = ps[:, 0:4, :].rearrange("p (s h) n -> p s h n", s=2)
        ps_max = ps[:, 4:6, :]
        ps_o = ps[:, 6, :]
        ps_misc = ps[:, 7, :]

        par = sb(top, "par", [P, NPAR])
        const = sb(top, "const", [P, NCONST])
        signs = [sb(top, f"signs{i}", [P, CB, TAPS, C], F16) for i in range(2)]
        proj_w = sb(top, "proj_w", [P, CB, C])
        ones = sb(top, "ones", [P, P])
        gn_a = sb(top, "gn_a", [P, B * CB])
        gn_b = sb(top, "gn_b", [P, B * CB])
        bound = sb(top, "bound", [P, 4])
        fscale = sb(top, "fscale", [P, 4])
        exp_scale = sb(top, "exp_scale", [P, 1])
        qk_bias = sb(top, "qk_bias", [P, 4])
        proj_bias = sb(top, "proj_bias", [P, CB])
        conv_scale = sb(top, "conv_scale", [P, 2])
        bn_st = sb(top, "bn_st", [P, CB, B * NB, 6])
        xt = sb(top, "xt", [P, 2, CB, TB])
        y32 = sb(top, "y32", [P, 2, 2, TB])

        x_used = sem("x_used")
        x_in = [sem("x_in0"), sem("x_in1")]
        pv_done = sem("pv_done")
        proj_ready = sem("proj_ready")
        conv_evac = sem("conv_evac")

        g = Shared()
        g.ps, g.ps_s, g.ps_max, g.ps_o, g.ps_misc, g.par, g.const = ps, ps_s, ps_max, ps_o, ps_misc, par, const
        g.signs, g.proj_w, g.ones, g.gn_a, g.gn_b, g.bound, g.fscale = signs, proj_w, ones, gn_a, gn_b, bound, fscale
        g.exp_scale, g.qk_bias, g.proj_bias, g.conv_scale, g.bn_st, g.xt, g.y32 = exp_scale, qk_bias, proj_bias, conv_scale, bn_st, xt, y32
        g.x_used, g.x_in, g.pv_done, g.proj_ready, g.conv_evac = x_used, x_in, pv_done, proj_ready, conv_evac
        prologue(nc, x, qkv_t, proj_t, w0_t, w1_t, par_d, const_d, g)
        attention(nc, x, qkv_t, x1_d, g)
        convolutions(nc, x1_d, out, g)


def prologue(nc, x, qkv_t, proj_t, w0_t, w1_t, par_d, const_d, g):
    par, const, ones = g.par, g.const, g.ones
    with ExitStack() as ctx:
        def sem(name):
            return ctx.enter_context(nc.semaphore(name))

        def sb(name, shape, dt=F32):
            return ctx.enter_context(nc.sbuf_tensor(name, shape, dt))

        xf = sb("xf", [P, B * CB, N])
        wf = [sb(f"wf{i}", [P, CB * TAPS * C]) for i in range(2)]
        wabs = sb("wabs", [P, CB * TAPS * C])
        wq = sb("wq", [P, 2, CB, 3, P])
        wq_abs = sb("wq_abs", [P, 2, CB, 3, P])
        gn_st = sb("gn_st", [P, B * CB, NB, 6])
        mv = sb("mv", [P, B * CB, 2])
        mvg = sb("mvg", [P, B * CB, 2])
        dev = sb("dev", [P, B * CB])
        var = sb("var", [P, B * CB])
        std = sb("std", [P, B * CB])
        tmp = sb("tmp", [P, B * CB])
        apar = sb("apar", [P, NPAR])
        xnb = sb("xnb", [P, CB])
        cbound = sb("cbound", [P, 2, CB])
        qkb = sb("qkb", [P, 4])
        loc = sb("loc", [P, 4])
        rb = sb("rb", [P, 4])
        wsum = sb("wsum", [P, 2])
        esum = sb("esum", [P, 2])

        par_in, const_in, wq_in, proj_in = sem("par_in"), sem("const_in"), sem("wq_in"), sem("proj_in")
        w_in = [sem("w0_in"), sem("w1_in")]
        xf_in = [sem(f"xf_in{i}") for i in range(B * CB)]
        small = sem("small")
        ones_set = sem("ones_set")
        wq_abs_ready, std_ready, wsum_ready = sem("wq_abs_ready"), sem("std_ready"), sem("wsum_ready")
        xnb_ready, mv_ready, dev_ready, var_ready = sem("xnb_ready"), sem("mv_ready"), sem("dev_ready"), sem("var_ready")
        loc_ready, bound_ready = sem("loc_ready"), sem("bound_ready")
        small_mm, gmean_mm, gdev_mm, wsum_mm = sem("small_mm"), sem("gmean_mm"), sem("gdev_mm"), sem("wsum_mm")
        block = ctx.enter_context(nc.Block())

        @block.sync
        def _(sp):
            for i in range(B * CB):
                sp.dma_start(xf[:, i, :], x[i // CB, i % CB]).then_inc(xf_in[i], 16)

        @block.scalar
        def _(act):
            act.dma_start(par[:], par_d).then_inc(par_in, 16)
            act.dma_start(const[:], const_d).then_inc(const_in, 16)
            act.dma_start(wq[:].rearrange("p h c j o -> p h (c j o)"),
                          qkv_t.rearrange("h p n -> p h n")).then_inc(wq_in, 16)
            act.dma_start(g.proj_w[:], proj_t.rearrange("c p o -> p c o")).then_inc(proj_in, 16)
            for i, w in enumerate((w0_t, w1_t)):
                act.dma_start(wf[i][:].rearrange("p (c n) -> p c n", c=CB),
                              w.rearrange("c p n -> p c n")).then_inc(w_in[i], 16)
            act.wait_ge(wq_in, 16)
            nc.scalar.activation(wq_abs[:], wq[:], ACT.Abs).then_inc(wq_abs_ready, 1)
            for i in range(2):
                act.wait_ge(w_in[i], 16)
                nc.scalar.activation(g.signs[i][:].rearrange("p c t o -> p (c t o)"), wf[i][:], ACT.Sign)
                if i:
                    act.wait_ge(wsum_ready, 1)
                nc.scalar.activation(wabs[:], wf[i][:], ACT.Abs, accum_out=wsum[:, i:i + 1]).then_inc(wsum_ready, 1)
            act.wait_ge(var_ready, 1)
            nc.scalar.activation(std[:], var[:], ACT.Sqrt).then_inc(std_ready, 1)

        @block.gpsimd
        def _(pool):
            nc.gpsimd.memset(ones[:], 1.0).then_inc(ones_set, 1)
            pool.wait_ge(loc_ready, 1)
            nc.gpsimd.partition_all_reduce(g.bound[:], loc[:], P, RMAX).then_inc(bound_ready, 1)

        @block.tensor
        def _(pe):
            mm = nc.tensor.matmul
            pe.wait_ge(wq_abs_ready, 1)
            pe.wait_ge(xnb_ready, 1)
            for j in range(2):
                for hp in range(2):
                    for c in range(CB):
                        mm(g.ps_misc[:, 2 * j + hp:2 * j + hp + 1], wq_abs[:, hp, c, j, :], xnb[:, c:c + 1],
                           start=(c == 0), stop=(c == CB - 1))
            pe.wait_ge(proj_in, 16)
            for m in range(CB):
                for c in range(CB):
                    last = mm(g.ps_misc[:, 4 + m:5 + m], g.proj_w[:, c, m * P:(m + 1) * P],
                              par[:, QKVB + 4 + c:QKVB + 5 + c], start=(c == 0), stop=(c == CB - 1))
            last.then_inc(small_mm, 1)
            pe.wait_ge(wsum_ready, 2)
            pe.wait_ge(ones_set, 1)
            mm(g.ps[:, 0, 0:2], ones[:], wsum[:], start=True, stop=True).then_inc(wsum_mm, 1)
            pe.wait_ge(const_in, 16)
            pe.wait_ge(mv_ready, 1)
            mm(g.ps[:, 1, 0:2 * B * CB], const[:, GAVG:GAVG + P], mv[:].rearrange("p a b -> p (a b)"),
               start=True, stop=True).then_inc(gmean_mm, 1)
            pe.wait_ge(dev_ready, 1)
            mm(g.ps[:, 2, 0:B * CB], const[:, GAVG:GAVG + P], dev[:], start=True, stop=True).then_inc(gdev_mm, 1)
            pe.sem_inc(g.pv_done, 1)
            pe.sem_inc(g.proj_ready, 4)

        @block.vector
        def _(dve):
            steps = [0]

            def step(ins):
                steps[0] += 1
                ins.then_inc(small, 1)
                dve.wait_ge(small, steps[0])

            v = nc.vector
            dve.wait_ge(par_in, 16)
            step(v.scalar_tensor_tensor(out=apar[:], in0=par[:], scalar=-1.0, in1=par[:], op0=ALU.mult, op1=ALU.max))
            v.scalar_tensor_tensor(out=xnb[:], in0=apar[:, GW:GW + 2], scalar=GN_MAX, in1=apar[:, GB:GB + 2],
                                   op0=ALU.mult, op1=ALU.add).then_inc(xnb_ready, 1)
            bn = apar[:, BN0:BN0 + 8].rearrange("p (l k c) -> p l k c", l=2, k=2)
            step(v.scalar_tensor_tensor(out=cbound[:], in0=bn[:, :, 0, :], scalar=BN_MAX, in1=bn[:, :, 1, :],
                                        op0=ALU.mult, op1=ALU.add))
            dve.wait_ge(small_mm, 1)
            step(v.tensor_tensor(qkb[:], g.ps_misc[:, 0:4], apar[:, QKVB:QKVB + 4], ALU.add))
            step(v.tensor_tensor(g.proj_bias[:], g.ps_misc[:, 4:6], par[:, PB:PB + 2], ALU.add))
            step(v.tensor_reduce(loc[:, 0:2], qkb[:].rearrange("p (j h) -> p j h", j=2), AX.X, ALU.max))
            v.tensor_reduce(loc[:, 2:4], cbound[:], AX.X, ALU.max).then_inc(loc_ready, 1)
            for i in range(B * CB):
                dve.wait_ge(xf_in[i], 16)
                for n in range(NB):
                    last = v.bn_stats(gn_st[:, i, n, :], xf[:, i, n * TB:(n + 1) * TB])
                step(last)
                last = v.bn_aggr(mv[:, i, :], gn_st[:, i].rearrange("p n s -> p (n s)"))
            last.then_inc(mv_ready, 1)
            dve.wait_ge(bound_ready, 1)
            step(v.tensor_scalar(g.bound[:], g.bound[:], 1e-6, None, ALU.max))
            step(v.reciprocal(rb[:], g.bound[:]))
            step(v.tensor_scalar(g.fscale[:], rb[:], RANGE, None, ALU.mult))
            step(v.tensor_scalar(g.exp_scale[:], g.bound[:, 0:1], g.bound[:, 1:2], 1.0 / (RANGE * RANGE * HD ** 0.5),
                                 ALU.mult, ALU.mult))
            step(v.tensor_scalar(g.qk_bias[:, 0:2], par[:, QKVB:QKVB + 2], g.fscale[:, 0:1], None, ALU.mult))
            step(v.tensor_scalar(g.qk_bias[:, 2:4], par[:, QKVB + 2:QKVB + 4], g.fscale[:, 1:2], None, ALU.mult))
            dve.wait_ge(wsum_mm, 1)
            step(v.tensor_scalar(esum[:], g.ps[:, 0, 0:2], 1.0 / (C * C * TAPS * RANGE), None, ALU.mult))
            step(v.tensor_tensor(g.conv_scale[:], esum[:], g.bound[:, 2:4], ALU.mult))
            dve.wait_ge(gmean_mm, 1)
            step(v.tensor_copy(mvg[:].rearrange("p a b -> p (a b)"), g.ps[:, 1, 0:2 * B * CB]))
            step(v.tensor_tensor(tmp[:], mv[:, :, 0], mvg[:, :, 0], ALU.subtract))
            v.tensor_tensor(dev[:], tmp[:], tmp[:], ALU.mult).then_inc(dev_ready, 1)
            dve.wait_ge(gdev_mm, 1)
            v.scalar_tensor_tensor(out=var[:], in0=g.ps[:, 2, 0:B * CB], scalar=GN_EPS, in1=mvg[:, :, 1],
                                   op0=ALU.add, op1=ALU.add).then_inc(var_ready, 1)
            dve.wait_ge(std_ready, 1)
            step(v.reciprocal(var[:], std[:]))
            for b in range(B):
                s = slice(b * CB, (b + 1) * CB)
                step(v.tensor_tensor(g.gn_a[:, s], var[:, s], par[:, GW:GW + 2], ALU.mult))
                step(v.tensor_tensor(tmp[:, s], mvg[:, s, 0], g.gn_a[:, s], ALU.mult))
                step(v.tensor_tensor(g.gn_b[:, s], par[:, GB:GB + 2], tmp[:, s], ALU.subtract))
            dve.sem_inc(g.x_used, 2)


def attention(nc, x, qkv_t, x1_d, g):
    xt, y32 = g.xt, g.y32
    ident = g.const[:, IDENT:IDENT + P]
    mask = g.const[0:QT, MASK:MASK + TB].rearrange("p (a n) -> p a n", a=QT)
    with ExitStack() as ctx:
        def sem(name):
            return ctx.enter_context(nc.semaphore(name))

        def sb(name, shape, dt=F32):
            return ctx.enter_context(nc.sbuf_tensor(name, shape, dt))

        k1 = [sb(f"k1{h}", [P, N], F16) for h in "ab"]
        k2 = [sb(f"k2{h}", [P, N], F16) for h in "ab"]
        q1 = [sb(f"q1{h}", [P, N], F16) for h in "ab"]
        q2 = [sb(f"q2{h}", [P, N], F16) for h in "ab"]
        vals = sb("vals", [P, KT, P])
        prob = sb("prob", [P, PBUF, 2 * TB])
        acc_dve = sb("acc_dve", [P, 2 * TB])
        acc_pool = sb("acc_pool", [P, 2 * TB])
        tot = sb("tot", [P, 2 * TB])
        o_raw = sb("o_raw", [P, TB])
        rec = sb("rec", [P, TB])
        o_all = sb("o_all", [P, CB, N])
        xn = sb("xn", [P, 2, CB, TB])
        wst = sb("wst", [P, CB, 3, P])
        pair_bias = sb("pair_bias", [P, 2])
        m_part = sb("m_part", [P, UNITS])
        m_max = sb("m_max", [P, 2 * QT])
        m_neg = sb("m_neg", [P, 2 * QT])
        x1t = sb("x1t", [P, 2, CB, TB])
        own = [slice(0, HD), slice(HD, P)]
        other = [slice(HD, P), slice(0, HD)]

        fixed_rows = sem("fixed_rows")
        w_staged = sem("w_staged")
        xn_ready = sem("xn_ready")
        y_ready = sem("y_ready")
        hi_ready = sem("hi_ready")
        split_done = sem("split_done")
        v_copied = sem("v_copied")
        s_ready = sem("s_ready")
        exp_done = sem("exp_done")
        dve_add, pool_add = sem("dve_add"), sem("pool_add")
        tot_ready = sem("tot_ready")
        sum_ready = sem("sum_ready")
        o_copied = sem("o_copied")
        rec_done = sem("rec_done")
        norm_done = sem("norm_done")
        mx_ready, mx_used = sem("mx_ready"), sem("mx_used")
        m_max_done = sem("m_max_done")
        m_neg_ready = sem("m_neg_ready")
        m_rows = sem("m_rows")
        q2_ready = sem("q2_ready")
        out_ready = sem("out_ready")
        x1_ready = sem("x1_ready")
        bias_ready = sem("bias_ready")
        x1_used = sem("x1_used")
        x1_out = [sem("x1_out0"), sem("x1_out1")]
        block = ctx.enter_context(nc.Block())

        def cols(i, n=TB):
            return bass.ds(i * n, n)

        @block.sync
        def _(sp):
            with sp.Fori(0, B) as b:
                with sp.Fori(0, 2) as hp:
                    sp.wait_ge(g.proj_ready, 4 + (b * 2 + hp) * (3 * NB))
                    sp.dma_start(wst[:].rearrange("p c j o -> p (c j o)"), qkv_t[bass.ds(hp, 1)].rearrange(
                        "h p n -> (h p) n")).then_inc(w_staged, 16)
                    with sp.Fori(0, NB // 2) as n2:
                        for s in range(2):
                            sp.wait_ge(g.x_used, 1 + s + b * 24 + hp * 8 + n2 * 2)
                            sp.dma_start(xt[:, s], x[bass.ds(b, 1), :, :, cols(n2 * 2 + s)].rearrange(
                                "b c p n -> p (b c) n")).then_inc(g.x_in[s], 16)
                with sp.Fori(0, NB // 2) as n2:
                    for s in range(2):
                        sp.wait_ge(g.x_used, 17 + s + b * 24 + n2 * 2)
                        sp.dma_start(xt[:, s], x[bass.ds(b, 1), :, :, cols(n2 * 2 + s)].rearrange(
                            "b c p n -> p (b c) n")).then_inc(g.x_in[s], 16)
                    for s in range(2):
                        sp.wait_ge(x1_ready, (b * NB + n2 * 2 + s + 3) * CB)
                        sp.dma_start(x1_d[bass.ds(b, 1), :, :, cols(n2 * 2 + s)].rearrange("b c p n -> p (b c) n"),
                                     x1t[:, s]).then_inc(x1_out[s], 16)
            for s in range(2):
                sp.wait_ge(x1_out[s], 16 + 16 * B * NB // 2)

        @block.gpsimd
        def _(pool):
            for h in range(2):
                nc.gpsimd.memset(q2[h][other[h], :], 0.0).then_inc(fixed_rows, 1)
                nc.gpsimd.memset(k2[h][other[h], :], 0.0).then_inc(fixed_rows, 1)
            pool.wait_ge(fixed_rows, 4)
            for h in range(2):
                s0 = other[h].start
                nc.gpsimd.memset(k2[h][s0:s0 + QT, :], SHIFT).then_inc(fixed_rows, 1)

            def sums(it):
                for j in range(1, KT // 2):
                    pool.wait_ge(exp_done, it * KT + (2 * j + 1))
                    if j == 1:
                        pool.wait_ge(tot_ready, it + 1)
                    else:
                        pool.wait_ge(pool_add, it * 15 + (j - 1))
                    a = prob[:, 0] if j == 1 else acc_pool[:]
                    nc.gpsimd.tensor_tensor(acc_pool[:], a, prob[:, 2 * j % PBUF], ALU.add).then_inc(pool_add, 1)
                pool.wait_ge(pool_add, it * 15 + 15)
                pool.wait_ge(dve_add, it * 15 + 15)
                nc.gpsimd.tensor_tensor(tot[:], acc_pool[:], acc_dve[:], ALU.add).then_inc(tot_ready, 1)

            pool.sem_inc(tot_ready, 1)
            with pool.Fori(0, B * 2) as pair:
                with pool.Fori(0, NB) as qb:
                    sums(pair * NB + qb)

        @block.scalar
        def _(act):
            def project(b, hp, n2, s):
                pn = (b * 2 + hp) * NB + n2 * 2 + s
                for j, dst in enumerate((q1, k1)):
                    act.wait_ge(g.proj_ready, 4 + pn * 3 + j + 1)
                    act.wait_ge(split_done, 8 + pn * 8)
                    nc.scalar.activation(y32[:, s, j], g.ps_s[:, s, j], ACT.Identity,
                                         bias=pair_bias[:, j:j + 1],
                                         scale=g.fscale[:, j:j + 1]).then_inc(y_ready, 1)
                    act.wait_ge(y_ready, pn * 2 + (j + 1))
                    for h in range(2):
                        last = nc.scalar.activation(dst[h][own[h], cols(n2 * 2 + s)], y32[own[h], s, j], ACT.Copy)
                    last.then_inc(hi_ready, 1)

            def softmax(it, first):
                for kt in range(KT):
                    act.wait_ge(s_ready, it * KT + (kt + 1))
                    if kt >= PBUF or not first:
                        act.wait_ge(g.pv_done, 1 + it * KT + (kt - PBUF + 1))
                        act.wait_ge(dve_add if kt % 2 else pool_add,
                                    it * 15 + (max((kt - PBUF) // 2, 1) if kt >= PBUF else kt // 2 - 1))
                    nc.scalar.activation(prob[:, kt % PBUF], g.ps_s[:, kt % 2].rearrange("p h n -> p (h n)"),
                                         ACT.Exp, scale=g.exp_scale[:]).then_inc(exp_done, 1)
                act.wait_ge(g.pv_done, 1 + it * KT + KT)
                if not first:
                    act.wait_ge(norm_done, it)
                nc.scalar.activation(o_raw[:], g.ps_o, ACT.Copy).then_inc(o_copied, 1)

            act.sem_inc(split_done, 16)
            with act.Fori(0, B) as b:
                with act.Fori(0, 2) as hp:
                    it0 = (b * 2 + hp) * NB
                    for j in range(2):
                        last = nc.scalar.activation(pair_bias[:, j:j + 1], g.qk_bias[:, bass.ds(hp + 2 * j, 1)], ACT.Copy)
                    last.then_inc(bias_ready, 1)
                    act.wait_ge(bias_ready, b * 2 + hp + 1)
                    act.wait_ge(g.pv_done, 1 + it0 * KT)
                    with act.Fori(0, NB // 2) as n2:
                        for s in range(2):
                            project(b, hp, n2, s)
                    softmax(it0, True)
                    with act.Fori(1, NB) as qb:
                        softmax(it0 + qb, False)

        @block.tensor
        def _(pe):
            mm = nc.tensor.matmul

            def project(b, hp, n2, s):
                pn = (b * 2 + hp) * NB + n2 * 2 + s
                pe.wait_ge(w_staged, 16 * (b * 2 + hp + 1))
                pe.wait_ge(xn_ready, (pn + 1) * CB)
                pe.wait_ge(split_done, 8 + pn * 8)
                for j in range(2):
                    for c in range(CB):
                        last = mm(g.ps_s[:, s, j], wst[:, c, j, :], xn[:, s, c, :], start=(c == 0), stop=(c == CB - 1))
                    last.then_inc(g.proj_ready, 1)
                pe.wait_ge(v_copied, 1 + pn)
                for t in range(QT):
                    for c in range(CB):
                        last = mm(g.ps_max[:, s, t * P:(t + 1) * P], xn[:, s, c, t * P:(t + 1) * P], wst[:, c, 2, :],
                                  start=(c == 0), stop=(c == CB - 1))
                last.then_inc(g.proj_ready, 1)

            def max_unit(it, qb, u):
                h, t, kb = u // (QT * NB), u // NB % QT, u % NB
                if u >= 2:
                    pe.wait_ge(mx_used, it * UNITS + (u - 1))
                mm(g.ps_max[:, u % 2], q1[h][:, bass.ds(qb * TB + t * P, P)], k1[h][:, kb * TB:(kb + 1) * TB],
                   start=True, stop=True).then_inc(mx_ready, 1)

            def max_rows(it):
                pe.wait_ge(m_neg_ready, it + 1)
                for h in range(2):
                    last = mm(g.ps_misc[0:QT, h * P:(h + 1) * P], m_neg[:, h * QT:(h + 1) * QT], ident,
                              start=True, stop=True)
                last.then_inc(m_rows, 1)

            def column_sums(it):
                pe.wait_ge(tot_ready, it + 2)
                for h in range(2):
                    last = mm(g.ps_misc[own[h], :], g.ones[:, 0:HD], tot[:, h * TB:(h + 1) * TB], start=True, stop=True)
                last.then_inc(sum_ready, 1)

            def values(it, kt, first):
                pe.wait_ge(exp_done, it * KT + (kt + 1))
                if kt == 0 and not first:
                    pe.wait_ge(o_copied, it)
                for h in range(2):
                    last = mm(g.ps_o[own[h], :], vals[:, kt, own[h]], prob[:, kt % PBUF, h * TB:(h + 1) * TB],
                              start=(kt == 0), stop=(kt == KT - 1))
                last.then_inc(g.pv_done, 1)

            def query_block(it, qb, first, with_max):
                pe.wait_ge(q2_ready, (it + 1) * 2)
                for kt in range(KT):
                    if kt >= 2 or not first:
                        pe.wait_ge(exp_done, it * KT + (kt - 1))
                    keys = slice(kt * P, (kt + 1) * P)
                    for h in range(2):
                        mm(g.ps_s[:, kt % 2, h], k1[h][:, keys], q1[h][:, cols(qb)], start=True, stop=False)
                        last = mm(g.ps_s[:, kt % 2, h], k2[h][:, keys], q2[h][:, cols(qb)], start=False, stop=True)
                    last.then_inc(s_ready, 1)
                    if with_max:
                        for u in units_of(kt):
                            max_unit(it + 1, qb + 1, u)
                    if kt:
                        values(it, kt - 1, first)
                    if kt == 5 and not first:
                        column_sums(it - 1)
                    if kt == 29 and with_max:
                        if not first:
                            pe.wait_ge(norm_done, it)
                        max_rows(it + 1)
                values(it, KT - 1, first)

            with pe.Fori(0, B) as b:
                with pe.Fori(0, 2) as hp:
                    it0 = (b * 2 + hp) * NB
                    with pe.Fori(0, NB // 2) as n2:
                        for s in range(2):
                            project(b, hp, n2, s)
                    pe.wait_ge(split_done, 16 + (it0 + NB) * 8)
                    pe.wait_ge(v_copied, 2 + it0 + NB)
                    pe.wait_ge(fixed_rows, 6)
                    for u in range(UNITS):
                        max_unit(it0, 0, u)
                    max_rows(it0)
                    query_block(it0, 0, True, True)
                    with pe.Fori(1, NB - 1) as qb:
                        query_block(it0 + qb, qb, False, True)
                    query_block(it0 + (NB - 1), NB - 1, False, False)
                    pe.wait_ge(norm_done, it0 + (NB - 1))
                    column_sums(it0 + (NB - 1))
                with pe.Fori(0, NB // 2) as n2:
                    for s in range(2):
                        pe.wait_ge(norm_done, (b + 1) * (2 * NB))
                        pe.wait_ge(x1_ready, (b * NB + n2 * 2 + s + 1) * CB)
                        for m in range(CB):
                            for c in range(CB):
                                last = mm(g.ps_s[:, s, m], g.proj_w[:, c, m * P:(m + 1) * P],
                                          o_all[:, c, cols(n2 * 2 + s)], start=(c == 0), stop=(c == CB - 1))
                        last.then_inc(out_ready, 1)

        @block.vector
        def _(dve):
            v = nc.vector
            dve.sem_inc(v_copied, 2)
            dve.sem_inc(x1_ready, 2 * CB)
            dve.sem_inc(x1_used, 2 * CB)
            for s in range(2):
                dve.sem_inc(x1_out[s], 16)

            def project(b, hp, n2, s):
                pn = (b * 2 + hp) * NB + n2 * 2 + s
                dve.wait_ge(g.x_in[s], 16 * (b * 12 + hp * 4 + n2 + 1))
                dve.wait_ge(g.proj_ready, 1 + pn * 3)
                for c in range(CB):
                    i = bass.ds(b * CB + c, 1)
                    v.tensor_scalar(xn[:, s, c], xt[:, s, c], g.gn_a[:, i], g.gn_b[:, i],
                                    ALU.mult, ALU.add).then_inc(xn_ready, 1)
                dve.wait_ge(xn_ready, (pn + 1) * CB)
                dve.sem_inc(g.x_used, 1)

            def split(b, hp, n2, s):
                pn = (b * 2 + hp) * NB + n2 * 2 + s
                here = cols(n2 * 2 + s)
                dve.wait_ge(g.pv_done, 1 + (b * 2 + hp) * (NB * KT))
                dve.wait_ge(hi_ready, pn * 2 + 1)
                for h in range(2):
                    v.tensor_tensor(q2[h][own[h], here], y32[own[h], s, 0], q1[h][own[h], here],
                                    ALU.subtract).then_inc(split_done, 1)
                    v.tensor_copy(q1[h][other[h], here], q1[h][own[h], here]).then_inc(split_done, 1)
                dve.wait_ge(hi_ready, pn * 2 + 2)
                for h in range(2):
                    v.tensor_tensor(k1[h][other[h], here], y32[own[h], s, 1], k1[h][own[h], here],
                                    ALU.subtract).then_inc(split_done, 1)
                    v.tensor_copy(k2[h][own[h], here], k1[h][own[h], here]).then_inc(split_done, 1)
                dve.wait_ge(g.proj_ready, 4 + (pn + 1) * 3)
                v.tensor_copy(vals[:, bass.ds((n2 * 2 + s) * QT, QT), :],
                              g.ps_max[:, s].rearrange("p (t d) -> p t d", t=QT)).then_inc(v_copied, 1)

            def max_unit(it, u):
                dve.wait_ge(mx_ready, it * UNITS + (u + 1))
                v.tensor_reduce(m_part[:, u:u + 1], g.ps_max[:, u % 2], AX.X, ALU.max).then_inc(mx_used, 1)

            def negate_max(it):
                dve.wait_ge(mx_used, it * UNITS + UNITS)
                v.tensor_reduce(m_max[:], m_part[:].rearrange("p (t k) -> p t k", k=NB), AX.X,
                                ALU.max).then_inc(m_max_done, 1)
                dve.wait_ge(m_max_done, it + 1)
                v.tensor_scalar(m_neg[:], m_max[:], -1.0 / SHIFT, None, ALU.mult).then_inc(m_neg_ready, 1)

            def write_max_rows(it, qb):
                dve.wait_ge(m_rows, it + 1)
                for h in range(2):
                    s0 = other[h].start
                    v.tensor_tensor(q2[h][s0:s0 + QT, cols(qb)].rearrange("p (a n) -> p a n", a=QT),
                                    g.ps_misc[0:QT, h * P:(h + 1) * P].unsqueeze(1).to_broadcast([QT, QT, P]),
                                    mask, ALU.mult).then_inc(q2_ready, 1)

            def normalize(it, hp, qb):
                dve.wait_ge(sum_ready, it + 1)
                dve.wait_ge(o_copied, it + 1)
                v.reciprocal(rec[:], g.ps_misc).then_inc(rec_done, 1)
                dve.wait_ge(rec_done, it + 1)
                v.tensor_tensor(o_all[:, bass.ds(hp, 1), cols(qb)].rearrange("p a n -> p (a n)"), o_raw[:], rec[:],
                                ALU.mult).then_inc(norm_done, 1)

            def query_block(it, hp, qb, first, with_max):
                for kt in range(KT + 1):
                    if with_max and kt < KT:
                        for u in units_of(kt):
                            max_unit(it + 1, u)
                    j = (kt - 2) // 2
                    if kt % 2 == 0 and j >= 1:
                        dve.wait_ge(exp_done, it * KT + kt)
                        if j == 1:
                            dve.wait_ge(tot_ready, it + 1)
                        if j > 1:
                            dve.wait_ge(dve_add, it * 15 + (j - 1))
                        a = prob[:, 1] if j == 1 else g_acc[:]
                        v.tensor_tensor(g_acc[:], a, prob[:, (kt - 1) % PBUF], ALU.add).then_inc(dve_add, 1)
                    if kt == 6 and not first:
                        normalize(it - 1, hp, qb - 1)
                    if kt == 27 and with_max:
                        negate_max(it + 1)
                    if kt == 29 and with_max:
                        write_max_rows(it + 1, qb + 1)

            g_acc = acc_dve
            with dve.Fori(0, B) as b:
                with dve.Fori(0, 2) as hp:
                    it0 = (b * 2 + hp) * NB
                    with dve.Fori(0, NB // 2) as n2:
                        for s in range(2):
                            project(b, hp, n2, s)
                        for s in range(2):
                            split(b, hp, n2, s)
                    for u in range(UNITS):
                        max_unit(it0, u)
                    negate_max(it0)
                    dve.wait_ge(fixed_rows, 6)
                    write_max_rows(it0, 0)
                    query_block(it0, hp, 0, True, True)
                    with dve.Fori(1, NB - 1) as qb:
                        query_block(it0 + qb, hp, qb, False, True)
                    query_block(it0 + (NB - 1), hp, NB - 1, False, False)
                    normalize(it0 + (NB - 1), hp, NB - 1)
                with dve.Fori(0, NB // 2) as n2:
                    for s in range(2):
                        nn = b * NB + n2 * 2 + s
                        dve.wait_ge(out_ready, nn + 1)
                        dve.wait_ge(g.x_in[s], 16 * (b * 12 + 8 + n2 + 1))
                        dve.wait_ge(x1_out[s], 16 * (b * (NB // 2) + n2 + 1))
                        dve.wait_ge(x1_used, (nn + 1) * CB)
                        for m in range(CB):
                            v.scalar_tensor_tensor(out=x1t[:, s, m], in0=g.ps_s[:, s, m],
                                                   scalar=g.proj_bias[:, m:m + 1], in1=xt[:, s, m],
                                                   op0=ALU.add, op1=ALU.add).then_inc(x1_ready, 1)
                        dve.wait_ge(x1_ready, (nn + 3) * CB)
                        for m in range(CB):
                            v.bn_stats(g.bn_st[:, m, bass.ds(nn, 1), :].rearrange("p a s -> p (a s)"),
                                       x1t[:, s, m]).then_inc(x1_used, 1)
                        dve.sem_inc(g.x_used, 1)


def convolutions(nc, x1_d, out, g):
    xt, y32 = g.xt, g.y32
    X0 = B * 3 * NB
    with ExitStack() as ctx:
        def sem(name):
            return ctx.enter_context(nc.semaphore(name))

        def sb(name, shape, dt=F32):
            return ctx.enter_context(nc.sbuf_tensor(name, shape, dt))

        a_hi = sb("a_hi", [P, CB, B, PW, PW], F16)
        a_lo = sb("a_lo", [P, CB, B, PW, PW], F16)
        hid = sb("hid", [P, CB, B, N])
        ot = sb("ot", [P, 2, CB, TB])
        bmv = sb("bmv", [P, CB, 2])
        bvar = sb("bvar", [P, CB])
        bstd = sb("bstd", [P, CB])
        brs = sb("brs", [P, CB])
        btmp = sb("btmp", [P, CB])
        bn_a = sb("bn_a", [P, 2, CB])
        bn_b = sb("bn_b", [P, 2, CB])

        border = sem("border")
        small = sem("bn_small")
        bvar_ready, bstd_ready, bn_ready = sem("bvar_ready"), sem("bstd_ready"), sem("bn_ready")
        relu_done = sem("relu_done")
        hi_done, lo_done = sem("hi_done"), sem("lo_done")
        conv_ready = sem("conv_ready")
        hid_stats = sem("hid_stats")
        ot_ready = sem("ot_ready")
        out_done = [sem("out_done0"), sem("out_done1")]
        block = ctx.enter_context(nc.Block())

        def cols(n):
            return bass.ds(n * TB, TB)

        @block.sync
        def _(sp):
            def load(l, b, n2, s):
                xl = X0 + (l * B + b) * NB + n2 * 2 + s
                sp.wait_ge(g.x_used, 1 + xl)
                sp.dma_start(xt[:, s], x1_d[bass.ds(b, 1), :, :, cols(n2 * 2 + s)].rearrange(
                    "b c p n -> p (b c) n")).then_inc(g.x_in[s], 16)

            with sp.Fori(0, B) as b:
                with sp.Fori(0, NB // 2) as n2:
                    for s in range(2):
                        load(0, b, n2, s)
            with sp.Fori(0, B) as b:
                with sp.Fori(0, NB // 2) as n2:
                    for s in range(2):
                        load(1, b, n2, s)
                    for s in range(2):
                        sp.wait_ge(ot_ready, (b * NB + n2 * 2 + s + 1) * CB)
                        sp.dma_start(out[bass.ds(b, 1), :, :, cols(n2 * 2 + s)].rearrange("b c p n -> p (b c) n"),
                                     ot[:, s]).then_inc(out_done[s], 16)
            for s in range(2):
                sp.wait_ge(out_done[s], 16 + 16 * B * NB // 2)

        @block.gpsimd
        def _(pool):
            for a in (a_hi, a_lo):
                for c in range(CB):
                    nc.gpsimd.memset(a[:, c, :, 0, :], 0.0).then_inc(border, 1)
                    nc.gpsimd.memset(a[:, c, :, PW - 1, :], 0.0).then_inc(border, 1)
                    nc.gpsimd.memset(a[:, c, :, 1:PW - 1, 0], 0.0).then_inc(border, 1)
                    nc.gpsimd.memset(a[:, c, :, 1:PW - 1, PW - 1], 0.0).then_inc(border, 1)

        @block.scalar
        def _(act):
            def relu(l, b, n2, s):
                t = (l * B + b) * NB + n2 * 2 + s
                if l == 0:
                    act.wait_ge(g.x_in[s], 16 * (X0 // 2 + b * (NB // 2) + n2 + 1))
                act.wait_ge(lo_done, 1 + t)
                for c in range(CB):
                    src = xt[:, s, c] if l == 0 else hid[:, c, bass.ds(b, 1), cols(n2 * 2 + s)].rearrange(
                        "p b n -> p (b n)")
                    nc.scalar.activation(y32[:, s, c], src, ACT.Relu, bias=bn_b[:, l, c:c + 1],
                                         scale=bn_a[:, l, c:c + 1]).then_inc(relu_done, 1)
                if l == 0:
                    act.wait_ge(relu_done, (t + 1) * CB)
                    act.sem_inc(g.x_used, 1)

            def evacuate(b, n):
                for m in range(CB):
                    act.wait_ge(conv_ready, (b * NB + n) * CB + (m + 1))
                    nc.scalar.activation(hid[:, m, bass.ds(b, 1), cols(n)].rearrange("p b n -> p (b n)"),
                                         g.ps[:, m, :], ACT.Copy, scale=g.conv_scale[:, 0:1]).then_inc(g.conv_evac, 1)

            act.sem_inc(lo_done, 2)
            for l in range(2):
                act.wait_ge(bvar_ready, l + 1)
                nc.scalar.activation(bstd[:], bvar[:], ACT.Sqrt).then_inc(bstd_ready, 1)
                act.wait_ge(bn_ready, l + 1)
                with act.Fori(0, B) as b:
                    for s in range(2):
                        relu(l, b, 0, s)
                    with act.Fori(0, NB // 2 - 1) as n2:
                        for s in range(2):
                            relu(l, b, n2 + 1, s)
                            if l == 0:
                                evacuate(b, n2 * 2 + s)
                    if l == 0:
                        for s in range(2):
                            evacuate(b, NB - 2 + s)

        @block.tensor
        def _(pe):
            def conv(l, b, n, last_rows):
                t = (l * B + b) * NB + n
                pe.wait_ge(lo_done, 2 + t + (1 if last_rows else 2))
                for m in range(CB):
                    pe.wait_ge(g.conv_evac, t * CB + m + 1)
                    k = 0
                    for c in range(CB):
                        for tap in range(TAPS):
                            for a in (a_hi, a_lo):
                                rows = bass.ds(n * ROWS + tap // 3, ROWS)
                                last = nc.tensor.matmul(
                                    g.ps[:, m, :], g.signs[l][:, c, tap, m * P:(m + 1) * P],
                                    a[:, c, bass.ds(b, 1), rows, tap % 3:tap % 3 + W].rearrange("p b r w -> p (b r) w"),
                                    start=(k == 0), stop=(k == CB * TAPS * 2 - 1))
                                k += 1
                    last.then_inc(conv_ready, 1)

            pe.sem_inc(g.conv_evac, 2)
            pe.wait_ge(border, 8 * CB)
            for l in range(2):
                with pe.Fori(0, B) as b:
                    with pe.Fori(0, NB - 1) as n:
                        conv(l, b, n, False)
                    conv(l, b, NB - 1, True)

        @block.vector
        def _(dve):
            v = nc.vector
            steps = [0]

            def step(ins):
                steps[0] += 1
                ins.then_inc(small, 1)
                dve.wait_ge(small, steps[0])

            def batch_norm(l):
                par, col = g.par, (BN0, BN1)[l]
                for m in range(CB):
                    step(v.bn_aggr(bmv[:, m, :], g.bn_st[:, m].rearrange("p n s -> p (n s)")))
                v.tensor_scalar(bvar[:], bmv[:, :, 1], BN_EPS, None, ALU.add).then_inc(bvar_ready, 1)
                dve.wait_ge(bstd_ready, l + 1)
                step(v.reciprocal(brs[:], bstd[:]))
                step(v.tensor_tensor(btmp[:], brs[:], par[:, col:col + 2], ALU.mult))
                step(v.tensor_scalar(bn_a[:, l, :], btmp[:], g.fscale[:, 2 + l:3 + l], None, ALU.mult))
                step(v.tensor_tensor(brs[:], bmv[:, :, 0], btmp[:], ALU.mult))
                step(v.tensor_tensor(btmp[:], par[:, col + 2:col + 4], brs[:], ALU.subtract))
                v.tensor_scalar(bn_b[:, l, :], btmp[:], g.fscale[:, 2 + l:3 + l], None, ALU.mult).then_inc(bn_ready, 1)

            def split(l, b, n2, s):
                t = (l * B + b) * NB + n2 * 2 + s
                dve.wait_ge(relu_done, (t + 1) * CB)
                for c in range(CB):
                    hi, lo = (a[:, c, bass.ds(b, 1), bass.ds((n2 * 2 + s) * ROWS + 1, ROWS), 1:W + 1].rearrange(
                        "p b r w -> p (b r) w") for a in (a_hi, a_lo))
                    y = y32[:, s, c].rearrange("p (r w) -> p r w", r=ROWS)
                    v.tensor_copy(hi, y).then_inc(hi_done, 1)
                    dve.wait_ge(hi_done, t * CB + (c + 1))
                    last = v.tensor_tensor(lo, y, hi, ALU.subtract)
                last.then_inc(lo_done, 1)

            def stats(b, n):
                for m in range(CB):
                    dve.wait_ge(g.conv_evac, 2 + (b * NB + n) * CB + (m + 1))
                    v.bn_stats(g.bn_st[:, m, bass.ds(b * NB + n, 1), :].rearrange("p a s -> p (a s)"),
                               hid[:, m, bass.ds(b, 1), cols(n)].rearrange("p b n -> p (b n)")).then_inc(hid_stats, 1)

            def finish(b, n2, s):
                t = b * NB + n2 * 2 + s
                dve.wait_ge(g.x_in[s], 16 * ((X0 + B * NB) // 2 + b * (NB // 2) + n2 + 1))
                dve.wait_ge(out_done[s], 16 * (b * (NB // 2) + n2 + 1))
                for m in range(CB):
                    dve.wait_ge(conv_ready, (B * NB + t) * CB + (m + 1))
                    v.scalar_tensor_tensor(out=ot[:, s, m], in0=g.ps[:, m, :], scalar=g.conv_scale[:, 1:2],
                                           in1=xt[:, s, m], op0=ALU.mult, op1=ALU.add).then_inc(ot_ready, 1)
                    dve.wait_ge(ot_ready, t * CB + (m + 1))
                    dve.sem_inc(g.conv_evac, 1)
                dve.sem_inc(g.x_used, 1)

            for s in range(2):
                dve.sem_inc(out_done[s], 16)
            for l in range(2):
                if l:
                    dve.wait_ge(hid_stats, B * NB * CB)
                batch_norm(l)
                with dve.Fori(0, B) as b:
                    for s in range(2):
                        split(l, b, 0, s)
                    with dve.Fori(0, NB // 2 - 1) as n2:
                        for s in range(2):
                            split(l, b, n2 + 1, s)
                            if l == 0:
                                stats(b, n2 * 2 + s)
                            else:
                                finish(b, n2, s)
                    for s in range(2):
                        if l == 0:
                            stats(b, NB - 2 + s)
                        else:
                            finish(b, NB // 2 - 1, s)


def constants():
    c = np.zeros((P, NCONST), np.float32)
    c[:, IDENT:IDENT + P] = np.eye(P)
    size = C // GROUPS
    c[:, GAVG:GAVG + P] = np.kron(np.eye(P // size), np.ones((size, size))) / size
    for t in range(QT):
        c[t, MASK + t * P:MASK + (t + 1) * P] = 1.0
    return c


def columns(*vectors):
    return np.ascontiguousarray(np.concatenate([np.asarray(v).reshape(-1, P) for v in vectors]).T)


def kernel(**inputs):
    import concourse.bacc as bacc
    from concourse.bass_utils import run_bass_kernel_spmd

    a = {k: np.asarray(v) for k, v in inputs.items()}
    arrays = {
        "x": np.ascontiguousarray(a["x"].reshape(B, CB, P, N)),
        "qkv_t": np.ascontiguousarray(
            a["L0_conv_qkv_weight"].reshape(3, 2, P, CB, P).transpose(1, 4, 3, 0, 2).reshape(2, P, CB * 3 * P)),
        "proj_t": np.ascontiguousarray(a["L0_conv_proj_weight"].T.reshape(CB, P, C)),
        "w0_t": np.ascontiguousarray(a["L1_conv_w0"].transpose(1, 2, 3, 0).reshape(CB, P, TAPS * C)),
        "w1_t": np.ascontiguousarray(a["L1_conv_w1"].transpose(1, 2, 3, 0).reshape(CB, P, TAPS * C)),
        "par": columns(a["L0_conv_gn_weight"], a["L0_conv_gn_bias"], a["L0_conv_qkv_bias"], a["L0_conv_proj_bias"],
                       a["L1_conv_gamma0"], a["L1_conv_beta0"], a["L1_conv_gamma1"], a["L1_conv_beta1"]),
        "const": constants(),
    }
    nc = bacc.Bacc("TRN2", target_bir_lowering=False, num_devices=1)
    args = [nc.dram_tensor(f"in_{k}", v.shape, F32, kind="ExternalInput").ap() for k, v in arrays.items()]
    args.append(nc.dram_tensor("out_y", (B, CB, P, N), F32, kind="ExternalOutput").ap())
    build(nc, *args)
    r = run_bass_kernel_spmd(nc, [{f"in_{k}": v for k, v in arrays.items()}], core_ids=[0])
    return r.results[0]["out_y"].reshape(B, C, H, W)
```

```python
from contextlib import ExitStack

import numpy as np

import concourse.bass as bass
from concourse import mybir

ALU = mybir.AluOpType
ACT = mybir.ActivationFunctionType
F32 = mybir.dt.float32
F16 = mybir.dt.float16
AX = mybir.AxisListType
RMAX = bass.bass_isa.ReduceOp.max

P = 128
B, C, H, W = 2, 256, 64, 64
CB = C // P
HEADS = 4
HD = C // HEADS
GROUPS = 32
N = H * W
TB = 512
NB = N // TB
KT = N // P
QT = TB // P
UNITS = 2 * QT * NB
PBUF = 4
TAPS = 9
PW = W + 2
ROWS = TB // W
EPS = 1e-5
GN_EPS = BN_EPS = EPS
SHIFT = 32768.0
RANGE = 4096.0
GN_MAX = float(np.sqrt(C // GROUPS * N))
BN_MAX = float(np.sqrt(B * N))

GW, GB, QKVB, PB, BN0, BN1 = 0, 2, 4, 10, 12, 16
NPAR = 20
IDENT, GAVG, MASK = 0, P, 2 * P
NCONST = 2 * P + TB


DVE_TILES = {False: [kt for kt in range(KT) if kt % 4 == 3], True: [kt for kt in range(KT) if kt % 2]}
POOL_TILES = {last: [kt for kt in range(KT) if kt not in DVE_TILES[last]] for last in (False, True)}
DVE_ADDS = {last: len(DVE_TILES[last]) for last in (False, True)}
POOL_ADDS = {last: len(POOL_TILES[last]) - 1 for last in (False, True)}
SPLITS = 4


THREE = [kt for kt in range(15) if kt % 4 in (1, 2)]


def units_of(kt):
    first = 2 * kt + sum(t < kt for t in THREE)
    if kt in THREE:
        return [first], [first + 1], [first + 2]
    return ([first], [], [first + 1]) if first < UNITS else ([], [], [])


NORM_PARTS = {kt: n for n, kt in enumerate((15, 17, 18, 19, 21, 22, 23, 25))}
NP = len(NORM_PARTS)


def adds_until(kt, last):
    if kt in DVE_TILES[last]:
        return DVE_TILES[last].index(kt) + 1
    return max(POOL_TILES[last].index(kt), 1)


def adds_before(adds, pair, qb):
    return pair * ((NB - 1) * adds[False] + adds[True]) + qb * adds[False]


class Shared:
    pass


def build(nc, x, qkv_t, proj_t, w0_t, w1_t, par_d, const_d, out):
    x1_d = nc.dram_tensor("x1_scratch", (B, CB, P, N), F32, kind="Internal").ap()
    with ExitStack() as top:
        def sem(name):
            return top.enter_context(nc.semaphore(name))

        def sb(stack, name, shape, dt=F32):
            return stack.enter_context(nc.sbuf_tensor(name, shape, dt))

        ps = top.enter_context(nc.psum_tensor("ps", [P, 8, TB], F32))
        ps_s = ps[:, 0:4, :].rearrange("p (s h) n -> p s h n", s=2)
        ps_max = ps[:, 4:6, :]
        ps_o = ps[:, 6, :]
        ps_misc = ps[:, 7, :]

        par = sb(top, "par", [P, NPAR])
        const = sb(top, "const", [P, NCONST])
        signs = [sb(top, f"signs{i}", [P, CB, TAPS, C], F16) for i in range(2)]
        proj_w = sb(top, "proj_w", [P, CB, C])
        ones = sb(top, "ones", [P, P])
        gn_a = sb(top, "gn_a", [P, B * CB])
        gn_b = sb(top, "gn_b", [P, B * CB])
        bound = sb(top, "bound", [P, 4])
        fscale = sb(top, "fscale", [P, 4])
        exp_scale = sb(top, "exp_scale", [P, 1])
        qk_bias = sb(top, "qk_bias", [P, 4])
        proj_bias = sb(top, "proj_bias", [P, CB])
        conv_scale = sb(top, "conv_scale", [P, 2])
        bn_st = sb(top, "bn_st", [P, CB, B * NB, 6])
        xt = sb(top, "xt", [P, 2, CB, TB])
        y32 = sb(top, "y32", [P, 2, 2, TB])

        x_used = sem("x_used")
        x_in = [sem("x_in0"), sem("x_in1")]
        pv_done = sem("pv_done")
        proj_ready = sem("proj_ready")
        conv_evac = sem("conv_evac")

        g = Shared()
        g.ps, g.ps_s, g.ps_max, g.ps_o, g.ps_misc, g.par, g.const = ps, ps_s, ps_max, ps_o, ps_misc, par, const
        g.signs, g.proj_w, g.ones, g.gn_a, g.gn_b, g.bound, g.fscale = signs, proj_w, ones, gn_a, gn_b, bound, fscale
        g.exp_scale, g.qk_bias, g.proj_bias, g.conv_scale, g.bn_st, g.xt, g.y32 = exp_scale, qk_bias, proj_bias, conv_scale, bn_st, xt, y32
        g.x_used, g.x_in, g.pv_done, g.proj_ready, g.conv_evac = x_used, x_in, pv_done, proj_ready, conv_evac
        prologue(nc, x, qkv_t, proj_t, w0_t, w1_t, par_d, const_d, g)
        attention(nc, x, qkv_t, x1_d, g)
        convolutions(nc, x1_d, out, g)


def prologue(nc, x, qkv_t, proj_t, w0_t, w1_t, par_d, const_d, g):
    par, const, ones = g.par, g.const, g.ones
    with ExitStack() as ctx:
        def sem(name):
            return ctx.enter_context(nc.semaphore(name))

        def sb(name, shape, dt=F32):
            return ctx.enter_context(nc.sbuf_tensor(name, shape, dt))

        xf = sb("xf", [P, B * CB, N])
        wf = [sb(f"wf{i}", [P, CB * TAPS * C]) for i in range(2)]
        wabs = sb("wabs", [P, CB * TAPS * C])
        wq = sb("wq", [P, 2, CB, 3, P])
        wq_abs = sb("wq_abs", [P, 2, CB, 3, P])
        gn_st = sb("gn_st", [P, B * CB, NB, 6])
        mv = sb("mv", [P, B * CB, 2])
        mvg = sb("mvg", [P, B * CB, 2])
        dev = sb("dev", [P, B * CB])
        var = sb("var", [P, B * CB])
        std = sb("std", [P, B * CB])
        tmp = sb("tmp", [P, B * CB])
        apar = sb("apar", [P, NPAR])
        xnb = sb("xnb", [P, CB])
        cbound = sb("cbound", [P, 2, CB])
        qkb = sb("qkb", [P, 4])
        loc = sb("loc", [P, 4])
        rb = sb("rb", [P, 4])
        wsum = sb("wsum", [P, 2])
        esum = sb("esum", [P, 2])

        par_in, const_in, wq_in, proj_in = sem("par_in"), sem("const_in"), sem("wq_in"), sem("proj_in")
        w_in = [sem("w0_in"), sem("w1_in")]
        xf_in = [sem(f"xf_in{i}") for i in range(B * CB)]
        small = sem("small")
        ones_set = sem("ones_set")
        wq_abs_ready, std_ready, wsum_ready = sem("wq_abs_ready"), sem("std_ready"), sem("wsum_ready")
        xnb_ready, mv_ready, dev_ready, var_ready = sem("xnb_ready"), sem("mv_ready"), sem("dev_ready"), sem("var_ready")
        loc_ready, bound_ready = sem("loc_ready"), sem("bound_ready")
        small_mm, gmean_mm, gdev_mm, wsum_mm = sem("small_mm"), sem("gmean_mm"), sem("gdev_mm"), sem("wsum_mm")
        block = ctx.enter_context(nc.Block())

        @block.sync
        def _(sp):
            for i in range(B * CB):
                sp.dma_start(xf[:, i, :], x[i // CB, i % CB]).then_inc(xf_in[i], 16)

        @block.scalar
        def _(act):
            act.dma_start(par[:], par_d).then_inc(par_in, 16)
            act.dma_start(const[:], const_d).then_inc(const_in, 16)
            act.dma_start(wq[:].rearrange("p h c j o -> p h (c j o)"),
                          qkv_t.rearrange("h p n -> p h n")).then_inc(wq_in, 16)
            act.dma_start(g.proj_w[:], proj_t.rearrange("c p o -> p c o")).then_inc(proj_in, 16)
            for i, w in enumerate((w0_t, w1_t)):
                act.dma_start(wf[i][:].rearrange("p (c n) -> p c n", c=CB),
                              w.rearrange("c p n -> p c n")).then_inc(w_in[i], 16)
            act.wait_ge(wq_in, 16)
            nc.scalar.activation(wq_abs[:], wq[:], ACT.Abs).then_inc(wq_abs_ready, 1)
            for i in range(2):
                act.wait_ge(w_in[i], 16)
                nc.scalar.activation(g.signs[i][:].rearrange("p c t o -> p (c t o)"), wf[i][:], ACT.Sign)
                if i:
                    act.wait_ge(wsum_ready, 1)
                nc.scalar.activation(wabs[:], wf[i][:], ACT.Abs, accum_out=wsum[:, i:i + 1]).then_inc(wsum_ready, 1)
            act.wait_ge(var_ready, 1)
            nc.scalar.activation(std[:], var[:], ACT.Sqrt).then_inc(std_ready, 1)

        @block.gpsimd
        def _(pool):
            nc.gpsimd.memset(ones[:], 1.0).then_inc(ones_set, 1)
            pool.wait_ge(loc_ready, 1)
            nc.gpsimd.partition_all_reduce(g.bound[:], loc[:], P, RMAX).then_inc(bound_ready, 1)

        @block.tensor
        def _(pe):
            mm = nc.tensor.matmul
            pe.wait_ge(wq_abs_ready, 1)
            pe.wait_ge(xnb_ready, 1)
            for j in range(2):
                for hp in range(2):
                    for c in range(CB):
                        mm(g.ps_misc[:, 2 * j + hp:2 * j + hp + 1], wq_abs[:, hp, c, j, :], xnb[:, c:c + 1],
                           start=(c == 0), stop=(c == CB - 1))
            pe.wait_ge(proj_in, 16)
            for m in range(CB):
                for c in range(CB):
                    last = mm(g.ps_misc[:, 4 + m:5 + m], g.proj_w[:, c, m * P:(m + 1) * P],
                              par[:, QKVB + 4 + c:QKVB + 5 + c], start=(c == 0), stop=(c == CB - 1))
            last.then_inc(small_mm, 1)
            pe.wait_ge(wsum_ready, 2)
            pe.wait_ge(ones_set, 1)
            mm(g.ps[:, 0, 0:2], ones[:], wsum[:], start=True, stop=True).then_inc(wsum_mm, 1)
            pe.wait_ge(const_in, 16)
            pe.wait_ge(mv_ready, 1)
            mm(g.ps[:, 1, 0:2 * B * CB], const[:, GAVG:GAVG + P], mv[:].rearrange("p a b -> p (a b)"),
               start=True, stop=True).then_inc(gmean_mm, 1)
            pe.wait_ge(dev_ready, 1)
            mm(g.ps[:, 2, 0:B * CB], const[:, GAVG:GAVG + P], dev[:], start=True, stop=True).then_inc(gdev_mm, 1)
            pe.sem_inc(g.pv_done, 1)
            pe.sem_inc(g.proj_ready, 4)

        @block.vector
        def _(dve):
            steps = [0]

            def step(ins):
                steps[0] += 1
                ins.then_inc(small, 1)
                dve.wait_ge(small, steps[0])

            v = nc.vector
            dve.wait_ge(par_in, 16)
            step(v.scalar_tensor_tensor(out=apar[:], in0=par[:], scalar=-1.0, in1=par[:], op0=ALU.mult, op1=ALU.max))
            v.scalar_tensor_tensor(out=xnb[:], in0=apar[:, GW:GW + 2], scalar=GN_MAX, in1=apar[:, GB:GB + 2],
                                   op0=ALU.mult, op1=ALU.add).then_inc(xnb_ready, 1)
            bn = apar[:, BN0:BN0 + 8].rearrange("p (l k c) -> p l k c", l=2, k=2)
            step(v.scalar_tensor_tensor(out=cbound[:], in0=bn[:, :, 0, :], scalar=BN_MAX, in1=bn[:, :, 1, :],
                                        op0=ALU.mult, op1=ALU.add))
            dve.wait_ge(small_mm, 1)
            step(v.tensor_tensor(qkb[:], g.ps_misc[:, 0:4], apar[:, QKVB:QKVB + 4], ALU.add))
            step(v.tensor_tensor(g.proj_bias[:], g.ps_misc[:, 4:6], par[:, PB:PB + 2], ALU.add))
            step(v.tensor_reduce(loc[:, 0:2], qkb[:].rearrange("p (j h) -> p j h", j=2), AX.X, ALU.max))
            v.tensor_reduce(loc[:, 2:4], cbound[:], AX.X, ALU.max).then_inc(loc_ready, 1)
            for i in range(B * CB):
                dve.wait_ge(xf_in[i], 16)
                for n in range(NB):
                    last = v.bn_stats(gn_st[:, i, n, :], xf[:, i, n * TB:(n + 1) * TB])
                step(last)
                last = v.bn_aggr(mv[:, i, :], gn_st[:, i].rearrange("p n s -> p (n s)"))
            last.then_inc(mv_ready, 1)
            dve.wait_ge(bound_ready, 1)
            step(v.tensor_scalar(g.bound[:], g.bound[:], 1e-6, None, ALU.max))
            step(v.reciprocal(rb[:], g.bound[:]))
            step(v.tensor_scalar(g.fscale[:], rb[:], RANGE, None, ALU.mult))
            step(v.tensor_scalar(g.exp_scale[:], g.bound[:, 0:1], g.bound[:, 1:2], 1.0 / (RANGE * RANGE * HD ** 0.5),
                                 ALU.mult, ALU.mult))
            step(v.tensor_scalar(g.qk_bias[:, 0:2], par[:, QKVB:QKVB + 2], g.fscale[:, 0:1], None, ALU.mult))
            step(v.tensor_scalar(g.qk_bias[:, 2:4], par[:, QKVB + 2:QKVB + 4], g.fscale[:, 1:2], None, ALU.mult))
            dve.wait_ge(wsum_mm, 1)
            step(v.tensor_scalar(esum[:], g.ps[:, 0, 0:2], 1.0 / (C * C * TAPS * RANGE), None, ALU.mult))
            step(v.tensor_tensor(g.conv_scale[:], esum[:], g.bound[:, 2:4], ALU.mult))
            dve.wait_ge(gmean_mm, 1)
            step(v.tensor_copy(mvg[:].rearrange("p a b -> p (a b)"), g.ps[:, 1, 0:2 * B * CB]))
            step(v.tensor_tensor(tmp[:], mv[:, :, 0], mvg[:, :, 0], ALU.subtract))
            v.tensor_tensor(dev[:], tmp[:], tmp[:], ALU.mult).then_inc(dev_ready, 1)
            dve.wait_ge(gdev_mm, 1)
            v.scalar_tensor_tensor(out=var[:], in0=g.ps[:, 2, 0:B * CB], scalar=GN_EPS, in1=mvg[:, :, 1],
                                   op0=ALU.add, op1=ALU.add).then_inc(var_ready, 1)
            dve.wait_ge(std_ready, 1)
            step(v.reciprocal(var[:], std[:]))
            for b in range(B):
                s = slice(b * CB, (b + 1) * CB)
                step(v.tensor_tensor(g.gn_a[:, s], var[:, s], par[:, GW:GW + 2], ALU.mult))
                step(v.tensor_tensor(tmp[:, s], mvg[:, s, 0], g.gn_a[:, s], ALU.mult))
                step(v.tensor_tensor(g.gn_b[:, s], par[:, GB:GB + 2], tmp[:, s], ALU.subtract))
            dve.sem_inc(g.x_used, 2)


def attention(nc, x, qkv_t, x1_d, g):
    xt, y32 = g.xt, g.y32
    ident = g.const[:, IDENT:IDENT + P]
    mask = g.const[0:QT, MASK:MASK + TB].rearrange("p (a n) -> p a n", a=QT)
    with ExitStack() as ctx:
        def sem(name):
            return ctx.enter_context(nc.semaphore(name))

        def sb(name, shape, dt=F32):
            return ctx.enter_context(nc.sbuf_tensor(name, shape, dt))

        k1 = [sb(f"k1{h}", [P, N], F16) for h in "ab"]
        k2 = [sb(f"k2{h}", [P, N], F16) for h in "ab"]
        q1 = [sb(f"q1{h}", [P, N], F16) for h in "ab"]
        q2 = [sb(f"q2{h}", [P, N], F16) for h in "ab"]
        vals = sb("vals", [P, KT, P])
        prob = sb("prob", [P, PBUF, 2 * TB])
        acc_dve = sb("acc_dve", [P, 2 * TB])
        acc_pool = sb("acc_pool", [P, 2 * TB])
        tot = sb("tot", [P, 2 * TB])
        o_raw = sb("o_raw", [P, TB])
        rec = sb("rec", [P, TB])
        o_all = sb("o_all", [P, CB, N])
        xn = sb("xn", [P, 2, CB, TB])
        wst = sb("wst", [P, CB, 3, P])
        pair_bias = sb("pair_bias", [P, 2])
        m_part = sb("m_part", [P, UNITS])
        m_max = sb("m_max", [P, 2 * QT])
        m_neg = sb("m_neg", [P, 2 * QT])
        x1t = sb("x1t", [P, 2, CB, TB])
        ps_v = [g.ps_o, g.ps_misc]
        own = [slice(0, HD), slice(HD, P)]
        other = [slice(HD, P), slice(0, HD)]

        fixed_rows = sem("fixed_rows")
        w_staged = sem("w_staged")
        xn_ready = sem("xn_ready")
        y_ready = sem("y_ready")
        hi_ready = sem("hi_ready")
        split_done = sem("split_done")
        qlo_done = sem("qlo_done")
        v_copied = sem("v_copied")
        s_ready = sem("s_ready")
        exp_done = sem("exp_done")
        dve_add, pool_add = sem("dve_add"), sem("pool_add")
        tot_ready = sem("tot_ready")
        sum_ready = sem("sum_ready")
        o_copied = sem("o_copied")
        rec_done = sem("rec_done")
        norm_done = sem("norm_done")
        mx_ready, mx_used = sem("mx_ready"), sem("mx_used")
        m_max_done = sem("m_max_done")
        m_neg_ready = sem("m_neg_ready")
        m_rows = sem("m_rows")
        q2_ready = sem("q2_ready")
        out_ready = sem("out_ready")
        x1_ready = sem("x1_ready")
        bias_ready = sem("bias_ready")
        x1_used = sem("x1_used")
        x1_out = [sem("x1_out0"), sem("x1_out1")]
        block = ctx.enter_context(nc.Block())

        def cols(i, n=TB):
            return bass.ds(i * n, n)

        @block.sync
        def _(sp):
            with sp.Fori(0, B) as b:
                with sp.Fori(0, 2) as hp:
                    sp.wait_ge(g.proj_ready, 4 + (b * 2 + hp) * (3 * NB))
                    sp.dma_start(wst[:].rearrange("p c j o -> p (c j o)"), qkv_t[bass.ds(hp, 1)].rearrange(
                        "h p n -> (h p) n")).then_inc(w_staged, 16)
                    with sp.Fori(0, NB // 2) as n2:
                        for s in range(2):
                            sp.wait_ge(g.x_used, 1 + s + b * 24 + hp * 8 + n2 * 2)
                            sp.dma_start(xt[:, s], x[bass.ds(b, 1), :, :, cols(n2 * 2 + s)].rearrange(
                                "b c p n -> p (b c) n")).then_inc(g.x_in[s], 16)
                with sp.Fori(0, NB // 2) as n2:
                    for s in range(2):
                        sp.wait_ge(g.x_used, 17 + s + b * 24 + n2 * 2)
                        sp.dma_start(xt[:, s], x[bass.ds(b, 1), :, :, cols(n2 * 2 + s)].rearrange(
                            "b c p n -> p (b c) n")).then_inc(g.x_in[s], 16)
                    for s in range(2):
                        sp.wait_ge(x1_ready, (b * NB + n2 * 2 + s + 3) * CB)
                        sp.dma_start(x1_d[bass.ds(b, 1), :, :, cols(n2 * 2 + s)].rearrange("b c p n -> p (b c) n"),
                                     x1t[:, s]).then_inc(x1_out[s], 16)
            for s in range(2):
                sp.wait_ge(x1_out[s], 16 + 16 * B * NB // 2)

        @block.gpsimd
        def _(pool):
            for h in range(2):
                nc.gpsimd.memset(q2[h][other[h], :], 0.0).then_inc(fixed_rows, 1)
                nc.gpsimd.memset(k2[h][other[h], :], 0.0).then_inc(fixed_rows, 1)
            pool.wait_ge(fixed_rows, 4)
            for h in range(2):
                s0 = other[h].start
                nc.gpsimd.memset(k2[h][s0:s0 + QT, :], SHIFT).then_inc(fixed_rows, 1)

            def split(b, hp, n2, s):
                pn = (b * 2 + hp) * NB + n2 * 2 + s
                pool.wait_ge(g.pv_done, 1 + (b * 2 + hp) * (NB * KT))
                pool.wait_ge(hi_ready, pn * 2 + 1)
                for h in range(2):
                    nc.gpsimd.tensor_tensor(q2[h][own[h], cols(n2 * 2 + s)], y32[own[h], s, 0],
                                            q1[h][own[h], cols(n2 * 2 + s)], ALU.subtract).then_inc(qlo_done, 1)

            def sums(pair, qb, first, last):
                it = pair * NB + qb
                tiles, base = POOL_TILES[last], adds_before(POOL_ADDS, pair, qb)
                for n in range(1, POOL_ADDS[last] + 1):
                    pool.wait_ge(exp_done, it * KT + (tiles[n] + 1))
                    if n > 1:
                        pool.wait_ge(pool_add, base + (n - 1))
                    elif first:
                        pool.wait_ge(sum_ready, it + 1)
                    else:
                        pool.wait_ge(tot_ready, pair * (NB - 1) + qb + 1)
                    a = prob[:, tiles[0] % PBUF] if n == 1 else acc_pool[:]
                    nc.gpsimd.tensor_tensor(acc_pool[:], a, prob[:, tiles[n] % PBUF], ALU.add).then_inc(pool_add, 1)
                if not last:
                    pool.wait_ge(pool_add, base + POOL_ADDS[last])
                    pool.wait_ge(dve_add, adds_before(DVE_ADDS, pair, qb) + DVE_ADDS[last])
                    nc.gpsimd.tensor_tensor(tot[:], acc_pool[:], acc_dve[:], ALU.add).then_inc(tot_ready, 1)

            pool.sem_inc(tot_ready, 1)
            pool.sem_inc(sum_ready, 1)
            pool.sem_inc(qlo_done, 4)
            with pool.Fori(0, B) as b:
                with pool.Fori(0, 2) as hp:
                    with pool.Fori(0, NB // 2) as n2:
                        for s in range(2):
                            split(b, hp, n2, s)
                    pair = b * 2 + hp
                    sums(pair, 0, True, False)
                    with pool.Fori(1, NB - 1) as qb:
                        sums(pair, qb, False, False)
                    sums(pair, NB - 1, False, True)

        @block.scalar
        def _(act):
            def project(b, hp, n2, s):
                pn = (b * 2 + hp) * NB + n2 * 2 + s
                for j, dst in enumerate((q1, k1)):
                    act.wait_ge(g.proj_ready, 4 + pn * 3 + j + 1)
                    if j:
                        act.wait_ge(split_done, SPLITS * (pn + 1))
                    else:
                        act.wait_ge(qlo_done, 2 + 2 * pn)
                    nc.scalar.activation(y32[:, s, j], g.ps_s[:, s, j], ACT.Identity,
                                         bias=pair_bias[:, j:j + 1],
                                         scale=g.fscale[:, j:j + 1]).then_inc(y_ready, 1)
                    act.wait_ge(y_ready, 4 + pn * 2 + (j + 1))
                    for h in range(2):
                        last = nc.scalar.activation(dst[h][own[h], cols(n2 * 2 + s)], y32[own[h], s, j], ACT.Copy)
                    if j:
                        for h in range(2):
                            last = nc.scalar.activation(k2[h][own[h], cols(n2 * 2 + s)], y32[own[h], s, j], ACT.Copy)
                    last.then_inc(hi_ready, 1)

            def softmax(pair, qb, first, last=False):
                it = pair * NB + qb
                for kt in range(KT):
                    act.wait_ge(s_ready, it * KT + (kt + 1))
                    if kt >= PBUF or not first:
                        act.wait_ge(g.pv_done, 1 + it * KT + (kt - PBUF + 1))
                        old, of_last = (kt - PBUF) % KT, last and kt >= PBUF
                        adder, adds = (dve_add, DVE_ADDS) if old in DVE_TILES[of_last] else (pool_add, POOL_ADDS)
                        n = adds_until(old, of_last) - (0 if kt >= PBUF else adds[False])
                        act.wait_ge(adder, adds_before(adds, pair, qb) + n)
                    nc.scalar.activation(prob[:, kt % PBUF], g.ps_s[:, kt % 2].rearrange("p h n -> p (h n)"),
                                         ACT.Exp, scale=g.exp_scale[:]).then_inc(exp_done, 1)
                act.wait_ge(g.pv_done, 1 + it * KT + KT)
                if not first:
                    act.wait_ge(norm_done, it * NP)
                nc.scalar.activation(o_raw[:], g.ps_o, ACT.Copy).then_inc(o_copied, 1)

            act.sem_inc(split_done, 2 * SPLITS)
            act.sem_inc(y_ready, 4)
            with act.Fori(0, B) as b:
                with act.Fori(0, 2) as hp:
                    it0 = (b * 2 + hp) * NB
                    for j in range(2):
                        last = nc.scalar.activation(pair_bias[:, j:j + 1], g.qk_bias[:, bass.ds(hp + 2 * j, 1)], ACT.Copy)
                    last.then_inc(bias_ready, 1)
                    act.wait_ge(bias_ready, b * 2 + hp + 1)
                    act.wait_ge(g.pv_done, 1 + it0 * KT)
                    with act.Fori(0, NB // 2) as n2:
                        for s in range(2):
                            project(b, hp, n2, s)
                    softmax(b * 2 + hp, 0, True)
                    with act.Fori(1, NB - 1) as qb:
                        softmax(b * 2 + hp, qb, False)
                    softmax(b * 2 + hp, NB - 1, False, True)

        @block.tensor
        def _(pe):
            mm = nc.tensor.matmul

            def project(b, hp, n2, s, maxima):
                it0 = (b * 2 + hp) * NB
                pn = it0 + n2 * 2 + s
                pe.wait_ge(w_staged, 16 * (b * 2 + hp + 1))
                pe.wait_ge(xn_ready, (pn + 1) * CB)
                pe.wait_ge(y_ready, 2 + pn * 2)
                for j in range(2):
                    for c in range(CB):
                        last = mm(g.ps_s[:, s, j], wst[:, c, j, :], xn[:, s, c, :], start=(c == 0), stop=(c == CB - 1))
                    last.then_inc(g.proj_ready, 1)
                    if maxima:
                        first_maxima(it0, n2 - 1, s, [2 * j, 2 * j + 1])
                pe.wait_ge(v_copied, 1 + pn)
                for t in range(QT):
                    for c in range(CB):
                        last = mm(ps_v[s][:, t * P:(t + 1) * P], xn[:, s, c, t * P:(t + 1) * P], wst[:, c, 2, :],
                                  start=(c == 0), stop=(c == CB - 1))
                    if maxima and t == 1:
                        first_maxima(it0, n2 - 1, s, [4, 5])
                last.then_inc(g.proj_ready, 1)
                if maxima:
                    first_maxima(it0, n2 - 1, s, [6, 7])

            def first_maxima(it, n2, s, units):
                if units[0] == 0:
                    pe.wait_ge(split_done, SPLITS * (it + n2 * 2 + s + 3))
                for n in units:
                    h, t = n // QT, n % QT
                    pe.wait_ge(mx_used, 1 + it * UNITS + (n2 * 2 + s) * (2 * QT) + n)
                    mm(g.ps_max[:, n % 2], q1[h][:, t * P:(t + 1) * P], k1[h][:, cols(n2 * 2 + s)],
                       start=True, stop=True).then_inc(mx_ready, 1)

            def next_maxima(it, qb, units):
                for u in units:
                    h, t, kb = u // (QT * NB), u // NB % QT, u % NB
                    pe.wait_ge(mx_used, 1 + it * UNITS + u)
                    mm(g.ps_max[:, u % 2], q1[h][:, bass.ds(qb * TB + t * P, P)], k1[h][:, kb * TB:(kb + 1) * TB],
                       start=True, stop=True).then_inc(mx_ready, 1)

            def max_rows(it):
                pe.wait_ge(m_neg_ready, it + 1)
                for h in range(2):
                    last = mm(g.ps_misc[0:QT, h * P:(h + 1) * P], m_neg[:, h * QT:(h + 1) * QT], ident,
                              start=True, stop=True)
                last.then_inc(m_rows, 1)

            def column_sums(pair, qb, last):
                if last:
                    pe.wait_ge(pool_add, adds_before(POOL_ADDS, pair, qb) + POOL_ADDS[True])
                    pe.wait_ge(dve_add, adds_before(DVE_ADDS, pair, qb) + DVE_ADDS[True])
                else:
                    pe.wait_ge(tot_ready, pair * (NB - 1) + qb + 2)
                parts = [acc_pool, acc_dve] if last else [tot]
                for part in parts:
                    for h in range(2):
                        ins = mm(g.ps_misc[own[h], :], g.ones[:, 0:HD], part[:, h * TB:(h + 1) * TB],
                                 start=(part is parts[0]), stop=(part is parts[-1]))
                ins.then_inc(sum_ready, 1)

            def values(it, kt, first):
                pe.wait_ge(exp_done, it * KT + (kt + 1))
                if kt == 0 and not first:
                    pe.wait_ge(o_copied, it)
                for h in range(2):
                    last = mm(g.ps_o[own[h], :], vals[:, kt, own[h]], prob[:, kt % PBUF, h * TB:(h + 1) * TB],
                              start=(kt == 0), stop=(kt == KT - 1))
                last.then_inc(g.pv_done, 1)

            def query_block(it, pair, qb, first, with_max):
                pe.wait_ge(q2_ready, (it + 1) * 2)
                for kt in range(KT):
                    if kt >= 2 or not first:
                        pe.wait_ge(exp_done, it * KT + (kt - 1))
                    keys = slice(kt * P, (kt + 1) * P)
                    for h in range(2):
                        if h and with_max:
                            next_maxima(it + 1, qb + 1, units_of(kt)[0])
                        mm(g.ps_s[:, kt % 2, h], k1[h][:, keys], q1[h][:, cols(qb)], start=True, stop=False)
                        last = mm(g.ps_s[:, kt % 2, h], k2[h][:, keys], q2[h][:, cols(qb)], start=False, stop=True)
                    last.then_inc(s_ready, 1)
                    if with_max:
                        next_maxima(it + 1, qb + 1, units_of(kt)[1])
                    if kt:
                        values(it, kt - 1, first)
                    if with_max:
                        next_maxima(it + 1, qb + 1, units_of(kt)[2])
                    if kt == 5 and not first:
                        column_sums(pair, qb - 1, False)
                    if kt == 29 and with_max:
                        if not first:
                            pe.wait_ge(norm_done, it * NP)
                        max_rows(it + 1)
                values(it, KT - 1, first)

            with pe.Fori(0, B) as b:
                with pe.Fori(0, 2) as hp:
                    pair = b * 2 + hp
                    it0 = pair * NB
                    for s in range(2):
                        project(b, hp, 0, s, False)
                    with pe.Fori(1, NB // 2) as n2:
                        for s in range(2):
                            project(b, hp, n2, s, True)
                    for s in range(2):
                        first_maxima(it0, NB // 2 - 1, s, range(2 * QT))
                    pe.wait_ge(qlo_done, 4 + 2 * (it0 + NB))
                    pe.wait_ge(v_copied, 2 + it0 + NB)
                    pe.wait_ge(fixed_rows, 6)
                    max_rows(it0)
                    query_block(it0, pair, 0, True, True)
                    with pe.Fori(1, NB - 1) as qb:
                        query_block(it0 + qb, pair, qb, False, True)
                    query_block(it0 + (NB - 1), pair, NB - 1, False, False)
                    pe.wait_ge(norm_done, (it0 + (NB - 1)) * NP)
                    column_sums(pair, NB - 1, True)
                with pe.Fori(0, NB // 2) as n2:
                    for s in range(2):
                        pe.wait_ge(norm_done, (b + 1) * (2 * NB * NP))
                        pe.wait_ge(x1_ready, (b * NB + n2 * 2 + s + 1) * CB)
                        for m in range(CB):
                            for c in range(CB):
                                last = mm(g.ps_s[:, s, m], g.proj_w[:, c, m * P:(m + 1) * P],
                                          o_all[:, c, cols(n2 * 2 + s)], start=(c == 0), stop=(c == CB - 1))
                        last.then_inc(out_ready, 1)

        @block.vector
        def _(dve):
            v = nc.vector
            dve.sem_inc(v_copied, 2)
            dve.sem_inc(mx_used, 2)
            dve.sem_inc(x1_ready, 2 * CB)
            dve.sem_inc(x1_used, 2 * CB)
            for s in range(2):
                dve.sem_inc(x1_out[s], 16)

            def project(b, hp, n2, s):
                pn = (b * 2 + hp) * NB + n2 * 2 + s
                dve.wait_ge(g.x_in[s], 16 * (b * 12 + hp * 4 + n2 + 1))
                dve.wait_ge(g.proj_ready, 1 + pn * 3)
                for c in range(CB):
                    i = bass.ds(b * CB + c, 1)
                    v.tensor_scalar(xn[:, s, c], xt[:, s, c], g.gn_a[:, i], g.gn_b[:, i],
                                    ALU.mult, ALU.add).then_inc(xn_ready, 1)
                dve.wait_ge(xn_ready, (pn + 1) * CB)
                dve.sem_inc(g.x_used, 1)

            def split_q(b, hp, n2, s):
                pn = (b * 2 + hp) * NB + n2 * 2 + s
                here = cols(n2 * 2 + s)
                dve.wait_ge(g.pv_done, 1 + (b * 2 + hp) * (NB * KT))
                dve.wait_ge(hi_ready, pn * 2 + 1)
                for h in range(2):
                    v.tensor_copy(q1[h][other[h], here], q1[h][own[h], here]).then_inc(split_done, 1)

            def split_k(b, hp, n2, s):
                pn = (b * 2 + hp) * NB + n2 * 2 + s
                here = cols(n2 * 2 + s)
                dve.wait_ge(hi_ready, pn * 2 + 2)
                for h in range(2):
                    v.tensor_tensor(k1[h][other[h], here], y32[own[h], s, 1], k1[h][own[h], here],
                                    ALU.subtract).then_inc(split_done, 1)

            def copy_v(b, hp, n2, s):
                pn = (b * 2 + hp) * NB + n2 * 2 + s
                dve.wait_ge(g.proj_ready, 4 + (pn + 1) * 3)
                v.tensor_copy(vals[:, bass.ds((n2 * 2 + s) * QT, QT), :],
                              ps_v[s].rearrange("p (t d) -> p t d", t=QT)).then_inc(v_copied, 1)

            def first_maxima(it, n2, s, units):
                for n in units:
                    dve.wait_ge(mx_ready, it * UNITS + (n2 * 2 + s) * (2 * QT) + (n + 1))
                    v.tensor_reduce(m_part[:, bass.ds(n2 * 2 + (n * NB + s), 1)], g.ps_max[:, n % 2], AX.X,
                                    ALU.max).then_inc(mx_used, 1)

            def project_step(b, hp, n2, s, last=False):
                it0 = (b * 2 + hp) * NB
                before, after = (n2 - 1 + s, 1 - s), (n2 + s, 1 - s)
                if not last:
                    project(b, hp, *after)
                first_maxima(it0, n2 - 1, s, [0, 1])
                split_q(b, hp, *before)
                first_maxima(it0, n2 - 1, s, [2, 3])
                split_k(b, hp, *before)
                first_maxima(it0, n2 - 1, s, [4, 5])
                copy_v(b, hp, *before)
                first_maxima(it0, n2 - 1, s, [6, 7])

            def next_maxima(it, units):
                for u in units:
                    dve.wait_ge(mx_ready, it * UNITS + (u + 1))
                    v.tensor_reduce(m_part[:, u:u + 1], g.ps_max[:, u % 2], AX.X, ALU.max).then_inc(mx_used, 1)

            def negate_max(it):
                dve.wait_ge(mx_used, 2 + it * UNITS + UNITS)
                v.tensor_reduce(m_max[:], m_part[:].rearrange("p (t k) -> p t k", k=NB), AX.X,
                                ALU.max).then_inc(m_max_done, 1)
                dve.wait_ge(m_max_done, it + 1)
                v.tensor_scalar(m_neg[:], m_max[:], -1.0 / SHIFT, None, ALU.mult).then_inc(m_neg_ready, 1)

            def write_max_rows(it, qb):
                dve.wait_ge(m_rows, it + 1)
                for h in range(2):
                    s0 = other[h].start
                    v.tensor_tensor(q2[h][s0:s0 + QT, cols(qb)].rearrange("p (a n) -> p a n", a=QT),
                                    g.ps_misc[0:QT, h * P:(h + 1) * P].unsqueeze(1).to_broadcast([QT, QT, P]),
                                    mask, ALU.mult).then_inc(q2_ready, 1)

            def normalize(it, hp, qb, part, parts):
                size = TB // parts
                c = slice(part * size, (part + 1) * size)
                if part == 0:
                    dve.wait_ge(sum_ready, it + 2)
                    dve.wait_ge(o_copied, it + 1)
                v.reciprocal(rec[:, c], g.ps_misc[:, c]).then_inc(rec_done, NP // parts)
                dve.wait_ge(rec_done, it * NP + (part + 1) * (NP // parts))
                v.tensor_tensor(o_all[:, bass.ds(hp, 1), bass.ds(qb * TB + part * size, size)].rearrange(
                    "p a n -> p (a n)"), o_raw[:, c], rec[:, c], ALU.mult).then_inc(norm_done, NP // parts)

            def query_block(it, pair, hp, qb, first, with_max):
                adds, tiles, base = 0, DVE_TILES[not with_max], adds_before(DVE_ADDS, pair, qb)
                for kt in range(KT + 1):
                    if with_max and kt < KT:
                        for units in units_of(kt):
                            next_maxima(it + 1, units)
                    if kt - 1 in tiles:
                        dve.wait_ge(exp_done, it * KT + kt)
                        tile = prob[:, (kt - 1) % PBUF]
                        if adds:
                            dve.wait_ge(dve_add, base + adds)
                            v.tensor_tensor(acc_dve[:], acc_dve[:], tile, ALU.add).then_inc(dve_add, 1)
                        else:
                            dve.wait_ge(sum_ready if first else tot_ready,
                                        it + 1 if first else pair * (NB - 1) + qb + 1)
                            v.tensor_copy(acc_dve[:], tile).then_inc(dve_add, 1)
                        adds += 1
                    if kt in NORM_PARTS and not first:
                        normalize(it - 1, hp, qb - 1, NORM_PARTS[kt], NP)
                    if kt == 27 and with_max:
                        negate_max(it + 1)
                    if kt == 29 and with_max:
                        write_max_rows(it + 1, qb + 1)

            with dve.Fori(0, B) as b:
                with dve.Fori(0, 2) as hp:
                    pair = b * 2 + hp
                    it0 = pair * NB
                    project(b, hp, 0, 0)
                    project(b, hp, 0, 1)
                    split_q(b, hp, 0, 0)
                    split_k(b, hp, 0, 0)
                    copy_v(b, hp, 0, 0)
                    project(b, hp, 1, 0)
                    with dve.Fori(1, NB // 2 - 1) as n2:
                        for s in range(2):
                            project_step(b, hp, n2, s)
                    project_step(b, hp, NB // 2 - 1, 0)
                    project_step(b, hp, NB // 2 - 1, 1, True)
                    split_q(b, hp, NB // 2 - 1, 1)
                    split_k(b, hp, NB // 2 - 1, 1)
                    copy_v(b, hp, NB // 2 - 1, 1)
                    for s in range(2):
                        first_maxima(it0, NB // 2 - 1, s, range(2 * QT))
                    negate_max(it0)
                    dve.wait_ge(fixed_rows, 6)
                    write_max_rows(it0, 0)
                    query_block(it0, pair, hp, 0, True, True)
                    with dve.Fori(1, NB - 1) as qb:
                        query_block(it0 + qb, pair, hp, qb, False, True)
                    query_block(it0 + (NB - 1), pair, hp, NB - 1, False, False)
                    normalize(it0 + (NB - 1), hp, NB - 1, 0, 1)
                with dve.Fori(0, NB // 2) as n2:
                    for s in range(2):
                        nn = b * NB + n2 * 2 + s
                        dve.wait_ge(out_ready, nn + 1)
                        dve.wait_ge(g.x_in[s], 16 * (b * 12 + 8 + n2 + 1))
                        dve.wait_ge(x1_out[s], 16 * (b * (NB // 2) + n2 + 1))
                        dve.wait_ge(x1_used, (nn + 1) * CB)
                        for m in range(CB):
                            v.scalar_tensor_tensor(out=x1t[:, s, m], in0=g.ps_s[:, s, m],
                                                   scalar=g.proj_bias[:, m:m + 1], in1=xt[:, s, m],
                                                   op0=ALU.add, op1=ALU.add).then_inc(x1_ready, 1)
                        dve.wait_ge(x1_ready, (nn + 3) * CB)
                        for m in range(CB):
                            v.bn_stats(g.bn_st[:, m, bass.ds(nn, 1), :].rearrange("p a s -> p (a s)"),
                                       x1t[:, s, m]).then_inc(x1_used, 1)
                        dve.sem_inc(g.x_used, 1)


def convolutions(nc, x1_d, out, g):
    xt, y32 = g.xt, g.y32
    X0 = B * 3 * NB
    with ExitStack() as ctx:
        def sem(name):
            return ctx.enter_context(nc.semaphore(name))

        def sb(name, shape, dt=F32):
            return ctx.enter_context(nc.sbuf_tensor(name, shape, dt))

        a_hi = sb("a_hi", [P, CB, B, PW, PW], F16)
        a_lo = sb("a_lo", [P, CB, B, PW, PW], F16)
        hid = sb("hid", [P, CB, B, N])
        ot = sb("ot", [P, 2, CB, TB])
        bmv = sb("bmv", [P, CB, 2])
        bvar = sb("bvar", [P, CB])
        bstd = sb("bstd", [P, CB])
        brs = sb("brs", [P, CB])
        btmp = sb("btmp", [P, CB])
        bn_a = sb("bn_a", [P, 2, CB])
        bn_b = sb("bn_b", [P, 2, CB])

        border = sem("border")
        small = sem("bn_small")
        bvar_ready, bstd_ready, bn_ready = sem("bvar_ready"), sem("bstd_ready"), sem("bn_ready")
        relu_done = sem("relu_done")
        hi_done, lo_done = sem("hi_done"), sem("lo_done")
        conv_ready = sem("conv_ready")
        hid_stats = sem("hid_stats")
        ot_ready = sem("ot_ready")
        out_done = [sem("out_done0"), sem("out_done1")]
        block = ctx.enter_context(nc.Block())

        def cols(n):
            return bass.ds(n * TB, TB)

        @block.sync
        def _(sp):
            def load(l, b, n2, s):
                xl = X0 + (l * B + b) * NB + n2 * 2 + s
                sp.wait_ge(g.x_used, 1 + xl)
                sp.dma_start(xt[:, s], x1_d[bass.ds(b, 1), :, :, cols(n2 * 2 + s)].rearrange(
                    "b c p n -> p (b c) n")).then_inc(g.x_in[s], 16)

            with sp.Fori(0, B) as b:
                with sp.Fori(0, NB // 2) as n2:
                    for s in range(2):
                        load(0, b, n2, s)
            with sp.Fori(0, B) as b:
                with sp.Fori(0, NB // 2) as n2:
                    for s in range(2):
                        load(1, b, n2, s)
                    for s in range(2):
                        sp.wait_ge(ot_ready, (b * NB + n2 * 2 + s + 1) * CB)
                        sp.dma_start(out[bass.ds(b, 1), :, :, cols(n2 * 2 + s)].rearrange("b c p n -> p (b c) n"),
                                     ot[:, s]).then_inc(out_done[s], 16)
            for s in range(2):
                sp.wait_ge(out_done[s], 16 + 16 * B * NB // 2)

        @block.gpsimd
        def _(pool):
            for a in (a_hi, a_lo):
                for c in range(CB):
                    nc.gpsimd.memset(a[:, c, :, 0, :], 0.0).then_inc(border, 1)
                    nc.gpsimd.memset(a[:, c, :, PW - 1, :], 0.0).then_inc(border, 1)
                    nc.gpsimd.memset(a[:, c, :, 1:PW - 1, 0], 0.0).then_inc(border, 1)
                    nc.gpsimd.memset(a[:, c, :, 1:PW - 1, PW - 1], 0.0).then_inc(border, 1)

        @block.scalar
        def _(act):
            def relu(l, b, n2, s):
                t = (l * B + b) * NB + n2 * 2 + s
                if l == 0:
                    act.wait_ge(g.x_in[s], 16 * (X0 // 2 + b * (NB // 2) + n2 + 1))
                act.wait_ge(lo_done, 1 + t)
                for c in range(CB):
                    src = xt[:, s, c] if l == 0 else hid[:, c, bass.ds(b, 1), cols(n2 * 2 + s)].rearrange(
                        "p b n -> p (b n)")
                    nc.scalar.activation(y32[:, s, c], src, ACT.Relu, bias=bn_b[:, l, c:c + 1],
                                         scale=bn_a[:, l, c:c + 1]).then_inc(relu_done, 1)
                if l == 0:
                    act.wait_ge(relu_done, (t + 1) * CB)
                    act.sem_inc(g.x_used, 1)

            def evacuate(b, n):
                for m in range(CB):
                    act.wait_ge(conv_ready, (b * NB + n) * CB + (m + 1))
                    nc.scalar.activation(hid[:, m, bass.ds(b, 1), cols(n)].rearrange("p b n -> p (b n)"),
                                         g.ps[:, m, :], ACT.Copy, scale=g.conv_scale[:, 0:1]).then_inc(g.conv_evac, 1)

            act.sem_inc(lo_done, 2)
            for l in range(2):
                act.wait_ge(bvar_ready, l + 1)
                nc.scalar.activation(bstd[:], bvar[:], ACT.Sqrt).then_inc(bstd_ready, 1)
                act.wait_ge(bn_ready, l + 1)
                with act.Fori(0, B) as b:
                    for s in range(2):
                        relu(l, b, 0, s)
                    with act.Fori(0, NB // 2 - 1) as n2:
                        for s in range(2):
                            relu(l, b, n2 + 1, s)
                            if l == 0:
                                evacuate(b, n2 * 2 + s)
                    if l == 0:
                        for s in range(2):
                            evacuate(b, NB - 2 + s)

        @block.tensor
        def _(pe):
            def conv(l, b, n, last_rows):
                t = (l * B + b) * NB + n
                pe.wait_ge(lo_done, 2 + t + (1 if last_rows else 2))
                for m in range(CB):
                    pe.wait_ge(g.conv_evac, t * CB + m + 1)
                    k = 0
                    for c in range(CB):
                        for tap in range(TAPS):
                            for a in (a_hi, a_lo):
                                rows = bass.ds(n * ROWS + tap // 3, ROWS)
                                last = nc.tensor.matmul(
                                    g.ps[:, m, :], g.signs[l][:, c, tap, m * P:(m + 1) * P],
                                    a[:, c, bass.ds(b, 1), rows, tap % 3:tap % 3 + W].rearrange("p b r w -> p (b r) w"),
                                    start=(k == 0), stop=(k == CB * TAPS * 2 - 1))
                                k += 1
                    last.then_inc(conv_ready, 1)

            pe.sem_inc(g.conv_evac, 2)
            pe.wait_ge(border, 8 * CB)
            for l in range(2):
                with pe.Fori(0, B) as b:
                    with pe.Fori(0, NB - 1) as n:
                        conv(l, b, n, False)
                    conv(l, b, NB - 1, True)

        @block.vector
        def _(dve):
            v = nc.vector
            steps = [0]

            def step(ins):
                steps[0] += 1
                ins.then_inc(small, 1)
                dve.wait_ge(small, steps[0])

            def batch_norm(l):
                par, col = g.par, (BN0, BN1)[l]
                for m in range(CB):
                    step(v.bn_aggr(bmv[:, m, :], g.bn_st[:, m].rearrange("p n s -> p (n s)")))
                v.tensor_scalar(bvar[:], bmv[:, :, 1], BN_EPS, None, ALU.add).then_inc(bvar_ready, 1)
                dve.wait_ge(bstd_ready, l + 1)
                step(v.reciprocal(brs[:], bstd[:]))
                step(v.tensor_tensor(btmp[:], brs[:], par[:, col:col + 2], ALU.mult))
                step(v.tensor_scalar(bn_a[:, l, :], btmp[:], g.fscale[:, 2 + l:3 + l], None, ALU.mult))
                step(v.tensor_tensor(brs[:], bmv[:, :, 0], btmp[:], ALU.mult))
                step(v.tensor_tensor(btmp[:], par[:, col + 2:col + 4], brs[:], ALU.subtract))
                v.tensor_scalar(bn_b[:, l, :], btmp[:], g.fscale[:, 2 + l:3 + l], None, ALU.mult).then_inc(bn_ready, 1)

            def split(l, b, n2, s):
                t = (l * B + b) * NB + n2 * 2 + s
                dve.wait_ge(relu_done, (t + 1) * CB)
                for c in range(CB):
                    hi, lo = (a[:, c, bass.ds(b, 1), bass.ds((n2 * 2 + s) * ROWS + 1, ROWS), 1:W + 1].rearrange(
                        "p b r w -> p (b r) w") for a in (a_hi, a_lo))
                    y = y32[:, s, c].rearrange("p (r w) -> p r w", r=ROWS)
                    v.tensor_copy(hi, y).then_inc(hi_done, 1)
                    dve.wait_ge(hi_done, t * CB + (c + 1))
                    last = v.tensor_tensor(lo, y, hi, ALU.subtract)
                last.then_inc(lo_done, 1)

            def stats(b, n):
                for m in range(CB):
                    dve.wait_ge(g.conv_evac, 2 + (b * NB + n) * CB + (m + 1))
                    v.bn_stats(g.bn_st[:, m, bass.ds(b * NB + n, 1), :].rearrange("p a s -> p (a s)"),
                               hid[:, m, bass.ds(b, 1), cols(n)].rearrange("p b n -> p (b n)")).then_inc(hid_stats, 1)

            def finish(b, n2, s):
                t = b * NB + n2 * 2 + s
                dve.wait_ge(g.x_in[s], 16 * ((X0 + B * NB) // 2 + b * (NB // 2) + n2 + 1))
                dve.wait_ge(out_done[s], 16 * (b * (NB // 2) + n2 + 1))
                for m in range(CB):
                    dve.wait_ge(conv_ready, (B * NB + t) * CB + (m + 1))
                    v.scalar_tensor_tensor(out=ot[:, s, m], in0=g.ps[:, m, :], scalar=g.conv_scale[:, 1:2],
                                           in1=xt[:, s, m], op0=ALU.mult, op1=ALU.add).then_inc(ot_ready, 1)
                    dve.wait_ge(ot_ready, t * CB + (m + 1))
                    dve.sem_inc(g.conv_evac, 1)
                dve.sem_inc(g.x_used, 1)

            for s in range(2):
                dve.sem_inc(out_done[s], 16)
            for l in range(2):
                if l:
                    dve.wait_ge(hid_stats, B * NB * CB)
                batch_norm(l)
                with dve.Fori(0, B) as b:
                    for s in range(2):
                        split(l, b, 0, s)
                    with dve.Fori(0, NB // 2 - 1) as n2:
                        for s in range(2):
                            split(l, b, n2 + 1, s)
                            if l == 0:
                                stats(b, n2 * 2 + s)
                            else:
                                finish(b, n2, s)
                    for s in range(2):
                        if l == 0:
                            stats(b, NB - 2 + s)
                        else:
                            finish(b, NB // 2 - 1, s)


def constants():
    c = np.zeros((P, NCONST), np.float32)
    c[:, IDENT:IDENT + P] = np.eye(P)
    size = C // GROUPS
    c[:, GAVG:GAVG + P] = np.kron(np.eye(P // size), np.ones((size, size))) / size
    for t in range(QT):
        c[t, MASK + t * P:MASK + (t + 1) * P] = 1.0
    return c


def columns(*vectors):
    return np.ascontiguousarray(np.concatenate([np.asarray(v).reshape(-1, P) for v in vectors]).T)


def kernel(**inputs):
    import concourse.bacc as bacc
    from concourse.bass_utils import run_bass_kernel_spmd

    a = {k: np.asarray(v) for k, v in inputs.items()}
    arrays = {
        "x": np.ascontiguousarray(a["x"].reshape(B, CB, P, N)),
        "qkv_t": np.ascontiguousarray(
            a["L0_conv_qkv_weight"].reshape(3, 2, P, CB, P).transpose(1, 4, 3, 0, 2).reshape(2, P, CB * 3 * P)),
        "proj_t": np.ascontiguousarray(a["L0_conv_proj_weight"].T.reshape(CB, P, C)),
        "w0_t": np.ascontiguousarray(a["L1_conv_w0"].transpose(1, 2, 3, 0).reshape(CB, P, TAPS * C)),
        "w1_t": np.ascontiguousarray(a["L1_conv_w1"].transpose(1, 2, 3, 0).reshape(CB, P, TAPS * C)),
        "par": columns(a["L0_conv_gn_weight"], a["L0_conv_gn_bias"], a["L0_conv_qkv_bias"], a["L0_conv_proj_bias"],
                       a["L1_conv_gamma0"], a["L1_conv_beta0"], a["L1_conv_gamma1"], a["L1_conv_beta1"]),
        "const": constants(),
    }
    nc = bacc.Bacc("TRN2", target_bir_lowering=False, num_devices=1)
    args = [nc.dram_tensor(f"in_{k}", v.shape, F32, kind="ExternalInput").ap() for k, v in arrays.items()]
    args.append(nc.dram_tensor("out_y", (B, CB, P, N), F32, kind="ExternalOutput").ap())
    build(nc, *args)
    r = run_bass_kernel_spmd(nc, [{f"in_{k}": v for k, v in arrays.items()}], core_ids=[0])
    return r.results[0]["out_y"].reshape(B, C, H, W)
```

```python
from contextlib import ExitStack

import numpy as np

import concourse.bass as bass
from concourse import mybir

ALU = mybir.AluOpType
ACT = mybir.ActivationFunctionType
F32 = mybir.dt.float32
F16 = mybir.dt.float16
AX = mybir.AxisListType
RMAX = bass.bass_isa.ReduceOp.max

P = 128
B, C, H, W = 2, 256, 64, 64
CB = C // P
HEADS = 4
HD = C // HEADS
GROUPS = 32
N = H * W
TB = 512
NB = N // TB
KT = N // P
QT = TB // P
UNITS = 2 * QT * NB
PBUF = 4
TAPS = 9
PW = W + 2
CR = 2 * TB // W
CT = CR * W
BLOCKS = H // CR
EPS = 1e-5
GN_EPS = BN_EPS = EPS
SHIFT = 32768.0
RANGE = 4096.0
GN_MAX = float(np.sqrt(C // GROUPS * N))
BN_MAX = float(np.sqrt(B * N))

GW, GB, QKVB, PB, BN0, BN1 = 0, 2, 4, 10, 12, 16
NPAR = 20
IDENT, GAVG, MASK = 0, P, 2 * P
NCONST = 2 * P + TB


POOL_TILES = {False: [kt for kt in range(KT) if kt % 4 != 3], True: [0, 1] + list(range(6, KT - 4, 3))}
DVE_TILES = {last: [kt for kt in range(KT) if kt not in POOL_TILES[last]] for last in (False, True)}
DVE_ADDS = {last: len(DVE_TILES[last]) for last in (False, True)}
POOL_ADDS = {last: len(POOL_TILES[last]) - 1 for last in (False, True)}

THREE = [kt for kt in range(16) if kt % 4 in (2, 3)]
LAST_UNIT = (UNITS - len(THREE)) // 2 - 1
ROWS_AT = LAST_UNIT + 2


def units_of(kt):
    first = 2 * kt + sum(t < kt for t in THREE)
    if kt in THREE:
        return [first], [first + 1], [first + 2]
    return ([first], [], [first + 1]) if first < UNITS else ([], [], [])


PER_BATCH = 2 * (NB - 2) + NB
NORM_PARTS = {kt: n for n, kt in enumerate((15, 17, 18, 19, 21, 22, 23, 25))}
NP = len(NORM_PARTS)


def adds_until(kt, last):
    if kt in DVE_TILES[last]:
        return DVE_TILES[last].index(kt) + 1
    return max(POOL_TILES[last].index(kt), 1)


def adds_before(adds, pair, qb):
    return pair * ((NB - 1) * adds[False] + adds[True]) + qb * adds[False]


class Shared:
    pass


def build(nc, x, qkv_t, proj_t, w0_t, w1_t, par_d, const_d, out):
    x1_d = nc.dram_tensor("x1_scratch", (B, CB, P, N), F32, kind="Internal").ap()
    with ExitStack() as top:
        def sem(name):
            return top.enter_context(nc.semaphore(name))

        def sb(stack, name, shape, dt=F32):
            return stack.enter_context(nc.sbuf_tensor(name, shape, dt))

        ps = top.enter_context(nc.psum_tensor("ps", [P, 8, TB], F32))
        ps_s = ps[:, 0:4, :].rearrange("p (s h) n -> p s h n", s=2)
        ps_max = ps[:, 4:6, :]
        ps_o = ps[:, 6, :]
        ps_misc = ps[:, 7, :]

        par = sb(top, "par", [P, NPAR])
        const = sb(top, "const", [P, NCONST])
        signs0 = sb(top, "signs0", [P, CB, TAPS, C], F16)
        wf = sb(top, "wf", [P, TAPS * C])
        wsum = sb(top, "wsum", [P, 2, CB])
        y_tile = sb(top, "y_tile", [P, 2, CB, TB])
        proj_w = sb(top, "proj_w", [P, CB, C])
        ones = sb(top, "ones", [P, P])
        gn_a = sb(top, "gn_a", [P, B * CB])
        gn_b = sb(top, "gn_b", [P, B * CB])
        bound = sb(top, "bound", [P, 4])
        fscale = sb(top, "fscale", [P, 4])
        exp_scale = sb(top, "exp_scale", [P, 1])
        qk_bias = sb(top, "qk_bias", [P, 4])
        proj_bias = sb(top, "proj_bias", [P, CB])
        bn_st = sb(top, "bn_st", [P, CB, B * NB, 6])
        xt = sb(top, "xt", [P, 2, CB, TB])

        x_used = sem("x_used")
        x_in = [sem("x_in0"), sem("x_in1")]
        y_out = [sem("y_out0"), sem("y_out1")]
        pv_done = sem("pv_done")
        proj_ready = sem("proj_ready")
        w_staged = sem("w_staged")
        wf_in, sign_done, wsum_ready = sem("wf_in"), sem("sign_done"), sem("wsum_ready")

        g = Shared()
        g.ps, g.ps_s, g.ps_max, g.ps_o, g.ps_misc, g.par, g.const = ps, ps_s, ps_max, ps_o, ps_misc, par, const
        g.signs0, g.wf, g.wsum, g.y_tile = signs0, wf, wsum, y_tile
        g.y_out, g.w_staged, g.wf_in, g.sign_done, g.wsum_ready = y_out, w_staged, wf_in, sign_done, wsum_ready
        g.proj_w, g.ones, g.gn_a, g.gn_b, g.bound, g.fscale = proj_w, ones, gn_a, gn_b, bound, fscale
        g.exp_scale, g.qk_bias, g.proj_bias, g.bn_st, g.xt = exp_scale, qk_bias, proj_bias, bn_st, xt
        g.x_used, g.x_in, g.pv_done, g.proj_ready = x_used, x_in, pv_done, proj_ready
        with ExitStack() as first:
            g.own = [slice(0, HD), slice(HD, P)]
            g.other = [slice(HD, P), slice(0, HD)]
            g.k2 = [sb(first, f"k2{h}", [P, N], F16) for h in "ab"]
            g.q2 = [sb(first, f"q2{h}", [P, N], F16) for h in "ab"]
            g.wst = sb(first, "wst", [P, CB, 3, P])
            g.y32 = sb(first, "y32", [P, 2, 2, TB])
            g.xn = sb(first, "xn", [P, 2, CB, TB])
            g.xn_in = [sem("xn_in0"), sem("xn_in1")]
            prologue(nc, x, qkv_t, proj_t, w0_t, par_d, const_d, g)
            attention(nc, x, qkv_t, w0_t, x1_d, g)
        convolutions(nc, x1_d, w1_t, out, g)


def sign_weights(nc, act, g, signs, layer, c):
    act.wait_ge(g.wf_in, 16 * (c + (layer * CB + 1)))
    nc.scalar.activation(signs[:, bass.ds(c, 1)].rearrange("p c t o -> p (c t o)"), g.wf[:],
                         ACT.Sign).then_inc(g.sign_done, 1)
    act.wait_ge(g.sign_done, c + (layer * CB + 1))
    nc.scalar.activation(g.wf[:], g.wf[:], ACT.Abs,
                         accum_out=g.wsum[:, layer, bass.ds(c, 1)]).then_inc(g.wsum_ready, 1)


def prologue(nc, x, qkv_t, proj_t, w0_t, par_d, const_d, g):
    par, const, ones = g.par, g.const, g.ones
    with ExitStack() as ctx:
        def sem(name):
            return ctx.enter_context(nc.semaphore(name))

        def sb(name, shape, dt=F32):
            return ctx.enter_context(nc.sbuf_tensor(name, shape, dt))

        xf = sb("xf", [P, B * CB, N])
        wq = sb("wq", [P, 2, CB, 3, P])
        wq_abs = sb("wq_abs", [P, 2, CB, 3, P])
        gn_st = sb("gn_st", [P, B * CB, NB, 6])
        mv = sb("mv", [P, B * CB, 2])
        mvg = sb("mvg", [P, B * CB, 2])
        dev = sb("dev", [P, B * CB])
        var = sb("var", [P, B * CB])
        std = sb("std", [P, B * CB])
        tmp = sb("tmp", [P, B * CB])
        spare = sb("spare", [P, B * CB])
        apar = sb("apar", [P, NPAR])
        xnb = sb("xnb", [P, CB])
        cbound = sb("cbound", [P, 2, CB])
        qkb = sb("qkb", [P, 4])
        loc = sb("loc", [P, 4])
        rb = sb("rb", [P, 4])

        par_in, const_in, wq_in, proj_in = sem("par_in"), sem("const_in"), sem("wq_in"), sem("proj_in")
        xf_in = [sem(f"xf_in{i}") for i in range(B * CB)]
        small = sem("small")
        wq_abs_ready, std_ready = sem("wq_abs_ready"), sem("std_ready")
        xnb_ready, mv_ready, dev_ready, var_ready = sem("xnb_ready"), sem("mv_ready"), sem("dev_ready"), sem("var_ready")
        loc_ready, bound_ready = sem("loc_ready"), sem("bound_ready")
        pool_set = sem("pool_set")
        small_mm, gmean_mm, gdev_mm = sem("small_mm"), sem("gmean_mm"), sem("gdev_mm")
        block = ctx.enter_context(nc.Block())

        @block.sync
        def _(sp):
            for i in range(B * CB):
                sp.dma_start(xf[:, i, :], x[i // CB, i % CB]).then_inc(xf_in[i], 16)
            for s in range(2):
                sp.dma_start(g.xn[:, s], x[0, :, :, s * TB:(s + 1) * TB].rearrange("c p n -> p c n")).then_inc(
                    g.xn_in[s], 16)
            sp.dma_start(g.wst[:].rearrange("p c j o -> p (c j o)"), qkv_t[0]).then_inc(g.w_staged, 16)
            sp.dma_start(g.wf[:], w0_t[0]).then_inc(g.wf_in, 16)

        @block.scalar
        def _(act):
            act.dma_start(par[:], par_d).then_inc(par_in, 16)
            act.dma_start(wq[:].rearrange("p h c j o -> p h (c j o)"),
                          qkv_t.rearrange("h p n -> p h n")).then_inc(wq_in, 16)
            act.dma_start(g.proj_w[:], proj_t.rearrange("c p o -> p c o")).then_inc(proj_in, 16)
            act.dma_start(const[:], const_d).then_inc(const_in, 16)
            act.wait_ge(wq_in, 16)
            nc.scalar.activation(wq_abs[:], wq[:], ACT.Abs).then_inc(wq_abs_ready, 1)
            act.wait_ge(var_ready, 1)
            nc.scalar.activation(std[:], var[:], ACT.Sqrt).then_inc(std_ready, 1)
            act.wait_ge(std_ready, 1)
            nc.scalar.activation(spare[:], std[:], ACT.Exp, scale=-1.0)

        @block.gpsimd
        def _(pool):
            nc.gpsimd.memset(ones[:], 1.0).then_inc(pool_set, 1)
            pool.wait_ge(pool_set, 1)
            for h in range(2):
                nc.gpsimd.memset(g.q2[h][g.other[h], :], 0.0).then_inc(pool_set, 1)
                nc.gpsimd.memset(g.k2[h][g.other[h], :], 0.0).then_inc(pool_set, 1)
            pool.wait_ge(pool_set, 5)
            for h in range(2):
                s0 = g.other[h].start
                nc.gpsimd.memset(g.k2[h][s0:s0 + QT, :], SHIFT).then_inc(pool_set, 1)
            pool.wait_ge(pool_set, 7)
            pool.wait_ge(loc_ready, 1)
            nc.gpsimd.partition_all_reduce(g.bound[:], loc[:], P, RMAX).then_inc(bound_ready, 1)

        @block.tensor
        def _(pe):
            mm = nc.tensor.matmul
            pe.wait_ge(wq_abs_ready, 1)
            pe.wait_ge(xnb_ready, 1)
            for j in range(2):
                for hp in range(2):
                    for c in range(CB):
                        mm(g.ps_misc[:, 2 * j + hp:2 * j + hp + 1], wq_abs[:, hp, c, j, :], xnb[:, c:c + 1],
                           start=(c == 0), stop=(c == CB - 1))
            pe.wait_ge(proj_in, 16)
            for m in range(CB):
                for c in range(CB):
                    last = mm(g.ps_misc[:, 4 + m:5 + m], g.proj_w[:, c, m * P:(m + 1) * P],
                              par[:, QKVB + 4 + c:QKVB + 5 + c], start=(c == 0), stop=(c == CB - 1))
            last.then_inc(small_mm, 1)
            pe.wait_ge(const_in, 16)
            pe.wait_ge(mv_ready, 1)
            mm(g.ps[:, 1, 0:2 * B * CB], const[:, GAVG:GAVG + P], mv[:].rearrange("p a b -> p (a b)"),
               start=True, stop=True).then_inc(gmean_mm, 1)
            pe.wait_ge(dev_ready, 1)
            mm(g.ps[:, 2, 0:B * CB], const[:, GAVG:GAVG + P], dev[:], start=True, stop=True).then_inc(gdev_mm, 1)
            pe.sem_inc(g.pv_done, 1)
            pe.sem_inc(g.proj_ready, 4)

        @block.vector
        def _(dve):
            steps = [0]

            def step(ins):
                steps[0] += 1
                ins.then_inc(small, 1)
                dve.wait_ge(small, steps[0])

            v = nc.vector
            dve.wait_ge(par_in, 16)
            step(v.scalar_tensor_tensor(out=apar[:], in0=par[:], scalar=-1.0, in1=par[:], op0=ALU.mult, op1=ALU.max))
            v.scalar_tensor_tensor(out=xnb[:], in0=apar[:, GW:GW + 2], scalar=GN_MAX, in1=apar[:, GB:GB + 2],
                                   op0=ALU.mult, op1=ALU.add).then_inc(xnb_ready, 1)
            bn = apar[:, BN0:BN0 + 8].rearrange("p (l k c) -> p l k c", l=2, k=2)
            step(v.scalar_tensor_tensor(out=cbound[:], in0=bn[:, :, 0, :], scalar=BN_MAX, in1=bn[:, :, 1, :],
                                        op0=ALU.mult, op1=ALU.add))

            def stats(i):
                dve.wait_ge(xf_in[i], 16)
                for n in range(NB):
                    last = v.bn_stats(gn_st[:, i, n, :], xf[:, i, n * TB:(n + 1) * TB])
                step(last)
                return v.bn_aggr(mv[:, i, :], gn_st[:, i].rearrange("p n s -> p (n s)"))

            for i in range(B * CB):
                last = stats(i)
            last.then_inc(mv_ready, 1)
            dve.wait_ge(small_mm, 1)
            step(v.tensor_tensor(qkb[:], g.ps_misc[:, 0:4], apar[:, QKVB:QKVB + 4], ALU.add))
            step(v.tensor_tensor(g.proj_bias[:], g.ps_misc[:, 4:6], par[:, PB:PB + 2], ALU.add))
            step(v.tensor_reduce(loc[:, 0:2], qkb[:].rearrange("p (j h) -> p j h", j=2), AX.X, ALU.max))
            v.tensor_reduce(loc[:, 2:4], cbound[:], AX.X, ALU.max).then_inc(loc_ready, 1)
            dve.wait_ge(gmean_mm, 1)
            step(v.tensor_copy(mvg[:].rearrange("p a b -> p (a b)"), g.ps[:, 1, 0:2 * B * CB]))
            step(v.tensor_tensor(tmp[:], mv[:, :, 0], mvg[:, :, 0], ALU.subtract))
            v.tensor_tensor(dev[:], tmp[:], tmp[:], ALU.mult).then_inc(dev_ready, 1)
            dve.wait_ge(bound_ready, 1)
            step(v.tensor_scalar(g.bound[:], g.bound[:], 1e-6, None, ALU.max))
            step(v.reciprocal(rb[:], g.bound[:]))
            step(v.tensor_scalar(g.fscale[:], rb[:], RANGE, None, ALU.mult))
            step(v.tensor_scalar(g.exp_scale[:], g.bound[:, 0:1], g.bound[:, 1:2], 1.0 / (RANGE * RANGE * HD ** 0.5),
                                 ALU.mult, ALU.mult))
            step(v.tensor_scalar(g.qk_bias[:, 0:2], par[:, QKVB:QKVB + 2], g.fscale[:, 0:1], None, ALU.mult))
            step(v.tensor_scalar(g.qk_bias[:, 2:4], par[:, QKVB + 2:QKVB + 4], g.fscale[:, 1:2], None, ALU.mult))
            dve.wait_ge(gdev_mm, 1)
            v.scalar_tensor_tensor(out=var[:], in0=g.ps[:, 2, 0:B * CB], scalar=GN_EPS, in1=mvg[:, :, 1],
                                   op0=ALU.add, op1=ALU.add).then_inc(var_ready, 1)
            dve.wait_ge(std_ready, 1)
            step(v.reciprocal(var[:], std[:]))
            for b in range(B):
                s = slice(b * CB, (b + 1) * CB)
                step(v.tensor_tensor(g.gn_a[:, s], var[:, s], par[:, GW:GW + 2], ALU.mult))
                step(v.tensor_tensor(tmp[:, s], mvg[:, s, 0], g.gn_a[:, s], ALU.mult))
                step(v.tensor_tensor(g.gn_b[:, s], par[:, GB:GB + 2], tmp[:, s], ALU.subtract))
            dve.sem_inc(g.x_used, 2)


def attention(nc, x, qkv_t, w0_t, x1_d, g):
    xt, y32, wst, x1t = g.xt, g.y32, g.wst, g.y_tile
    k2, q2, own, other, xn = g.k2, g.q2, g.own, g.other, g.xn
    ident = g.const[:, IDENT:IDENT + P]
    mask = g.const[0:QT, MASK:MASK + TB].rearrange("p (a n) -> p a n", a=QT)
    with ExitStack() as ctx:
        def sem(name):
            return ctx.enter_context(nc.semaphore(name))

        def sb(name, shape, dt=F32):
            return ctx.enter_context(nc.sbuf_tensor(name, shape, dt))

        k1 = [sb(f"k1{h}", [P, N], F16) for h in "ab"]
        q1 = [sb(f"q1{h}", [P, N], F16) for h in "ab"]
        vals = sb("vals", [P, KT, P])
        prob = sb("prob", [P, PBUF, 2 * TB])
        acc_dve = sb("acc_dve", [P, 2 * TB])
        acc_pool = sb("acc_pool", [P, 2 * TB])
        tot = sb("tot", [P, 2 * TB])
        o_raw = sb("o_raw", [P, TB])
        rec = sb("rec", [P, TB])
        o_all = sb("o_all", [P, CB, N])
        pair_bias = sb("pair_bias", [P, 2])
        pair_gn = sb("pair_gn", [P, 2, CB])
        m_part = sb("m_part", [P, UNITS])
        m_max = sb("m_max", [P, 2 * QT])
        m_neg = sb("m_neg", [P, 2 * QT])
        ps_v = [g.ps_o, g.ps_misc]

        xn_ready = sem("xn_ready")
        xn_begun = sem("xn_begun")
        y_ready = sem("y_ready")
        hi_ready = sem("hi_ready")
        qhi_copied = sem("qhi_copied")
        qlo_done, klo_done = sem("qlo_done"), sem("klo_done")
        v_copied = sem("v_copied")
        s_ready = sem("s_ready")
        exp_done = sem("exp_done")
        dve_add, pool_add = sem("dve_add"), sem("pool_add")
        tot_ready = sem("tot_ready")
        sum_ready = sem("sum_ready")
        o_copied = sem("o_copied")
        rec_done = sem("rec_done")
        norm_done = sem("norm_done")
        mx_ready, mx_used = sem("mx_ready"), sem("mx_used")
        m_max_done = sem("m_max_done")
        m_neg_ready = sem("m_neg_ready")
        m_rows = sem("m_rows")
        q2_ready = sem("q2_ready")
        out_ready = sem("out_ready")
        x1_ready = sem("x1_ready")
        bias_ready = sem("bias_ready")
        x1_used = sem("x1_used")
        block = ctx.enter_context(nc.Block())

        def cols(i, n=TB):
            return bass.ds(i * n, n)

        @block.sync
        def _(sp):
            def load(src, b, n, s, used):
                sp.wait_ge(g.x_used, used)
                sp.dma_start(xt[:, s], src[b, :, :, cols(n)].rearrange("c p n -> p c n")).then_inc(g.x_in[s], 16)

            def store(b, n, s):
                sp.wait_ge(x1_ready, (b * NB + n + 3) * CB)
                sp.dma_start(x1_d[b, :, :, cols(n)].rearrange("c p n -> p c n"), x1t[:, s]).then_inc(g.y_out[s], 16)

            for b in range(B):
                before = b * PER_BATCH
                for hp in range(2):
                    pair = b * 2 + hp
                    with sp.Fori(1, NB // 2) as n2:
                        for s in range(2):
                            load(x, b, n2 * 2 + s, s, n2 * 2 + (before + hp * (NB - 2) + s - 1))
                    if pair < B * 2 - 1:
                        sp.wait_ge(g.proj_ready, 4 + (pair + 1) * (3 * NB))
                        sp.dma_start(wst[:].rearrange("p c j o -> p (c j o)"),
                                     qkv_t[1 - hp]).then_inc(g.w_staged, 16)
                        for s in range(2):
                            sp.dma_start(xn[:, s], x[(pair + 1) // 2, :, :, s * TB:(s + 1) * TB].rearrange(
                                "c p n -> p c n")).then_inc(g.xn_in[s], 16)
                before += 2 * (NB - 2)
                for s in range(2):
                    load(x, b, s, s, 1 + s + before)
                with sp.Fori(1, NB // 2) as n2:
                    for s in range(2):
                        load(x, b, n2 * 2 + s, s, n2 * 2 + (before + 1 + s))
                        store(b, (n2 - 1) * 2 + s, s)
                if b < B - 1:
                    sp.wait_ge(g.wsum_ready, b + 1)
                    sp.dma_start(g.wf[:], w0_t[b + 1]).then_inc(g.wf_in, 16)
                for s in range(2):
                    store(b, NB - 2 + s, s)

        @block.gpsimd
        def _(pool):
            def split(b, hp, n2, s):
                pn = (b * 2 + hp) * NB + n2 * 2 + s
                pool.wait_ge(g.pv_done, 1 + (b * 2 + hp) * (NB * KT))
                pool.wait_ge(hi_ready, pn * 2 + 1)
                for h in range(2):
                    nc.gpsimd.tensor_tensor(q2[h][own[h], cols(n2 * 2 + s)], y32[own[h], s, 0],
                                            q1[h][own[h], cols(n2 * 2 + s)], ALU.subtract).then_inc(qlo_done, 1)

            def split_k(b, hp, n2, s):
                pn = (b * 2 + hp) * NB + n2 * 2 + s
                pool.wait_ge(hi_ready, pn * 2 + 2)
                for h in range(2):
                    nc.gpsimd.tensor_tensor(k1[h][own[h], cols(n2 * 2 + s)], y32[own[h], s, 1],
                                            k2[h][own[h], cols(n2 * 2 + s)], ALU.subtract).then_inc(klo_done, 1)

            def normalize_input(b, hp, n2, s):
                pn = (b * 2 + hp) * NB + n2 * 2 + s
                pool.wait_ge(g.x_in[s], b * (8 * PER_BATCH) + hp * (8 * (NB - 2)) + n2 * 16)
                pool.wait_ge(g.proj_ready, 1 + pn * 3)
                pool.wait_ge(qlo_done, 2 + 2 * pn)
                pool.wait_ge(klo_done, 2 * pn)
                pool.sem_inc(xn_begun, 1)
                for c in range(CB):
                    nc.gpsimd.tensor_scalar(xn[:, s, c], xt[:, s, c], pair_gn[:, 0, c:c + 1], pair_gn[:, 1, c:c + 1],
                                            ALU.mult, ALU.add).then_inc(xn_ready, 1)
                pool.wait_ge(xn_ready, (pn + 1) * CB)
                pool.wait_ge(g.x_used, b * PER_BATCH + hp * (NB - 2) + n2 * 2 + s)
                pool.sem_inc(g.x_used, 1)

            def sums(pair, qb, first, last):
                it = pair * NB + qb
                tiles, base = POOL_TILES[last], adds_before(POOL_ADDS, pair, qb)
                for n in range(1, POOL_ADDS[last] + 1):
                    pool.wait_ge(exp_done, it * KT + (tiles[n] + 1))
                    if n > 1:
                        pool.wait_ge(pool_add, base + (n - 1))
                    elif first:
                        pool.wait_ge(sum_ready, it + 1)
                    else:
                        pool.wait_ge(tot_ready, pair * (NB - 1) + qb + 1)
                    a = prob[:, tiles[0] % PBUF] if n == 1 else acc_pool[:]
                    nc.gpsimd.tensor_tensor(acc_pool[:], a, prob[:, tiles[n] % PBUF], ALU.add).then_inc(pool_add, 1)
                if not last:
                    pool.wait_ge(pool_add, base + POOL_ADDS[last])
                    pool.wait_ge(dve_add, adds_before(DVE_ADDS, pair, qb) + DVE_ADDS[last])
                    nc.gpsimd.tensor_tensor(tot[:], acc_pool[:], acc_dve[:], ALU.add).then_inc(tot_ready, 1)

            pool.sem_inc(tot_ready, 1)
            pool.sem_inc(sum_ready, 1)
            pool.sem_inc(qlo_done, 4)
            pool.sem_inc(klo_done, 4)
            with pool.Fori(0, B) as b:
                with pool.Fori(0, 2) as hp:
                    pair = b * 2 + hp
                    with pool.Fori(0, NB // 2 - 1) as n2:
                        for s in range(2):
                            split(b, hp, n2, s)
                            pool.wait_ge(xn_ready, (pair * NB + 2) * CB)
                            normalize_input(b, hp, n2 + 1, s)
                            split_k(b, hp, n2, s)
                    for s in range(2):
                        split(b, hp, NB // 2 - 1, s)
                        split_k(b, hp, NB // 2 - 1, s)
                    sums(pair, 0, True, False)
                    with pool.Fori(1, NB - 1) as qb:
                        sums(pair, qb, False, False)
                    sums(pair, NB - 1, False, True)

        @block.scalar
        def _(act):
            def project(b, hp, n2, s):
                pn = (b * 2 + hp) * NB + n2 * 2 + s
                for j in range(2):
                    act.wait_ge(g.proj_ready, 4 + pn * 3 + j + 1)
                    act.wait_ge(klo_done if j else qlo_done, 2 + 2 * pn)
                    nc.scalar.activation(y32[:, s, j], g.ps_s[:, s, j], ACT.Identity,
                                         bias=pair_bias[:, j:j + 1],
                                         scale=g.fscale[:, j:j + 1]).then_inc(y_ready, 1)
                    act.wait_ge(y_ready, 4 + pn * 2 + (j + 1))
                    for h in range(2):
                        for dst in ((k2[h][own[h]], k1[h][other[h]]) if j else (q1[h][own[h]],)):
                            last = nc.scalar.activation(dst[:, cols(n2 * 2 + s)], y32[own[h], s, j], ACT.Copy)
                    last.then_inc(hi_ready, 1)

            def softmax(pair, qb, first, last=False):
                it = pair * NB + qb
                for kt in range(KT):
                    act.wait_ge(s_ready, it * KT + (kt + 1))
                    if kt >= PBUF or not first:
                        act.wait_ge(g.pv_done, 1 + it * KT + (kt - PBUF + 1))
                        old, of_last = (kt - PBUF) % KT, last and kt >= PBUF
                        adder, adds = (dve_add, DVE_ADDS) if old in DVE_TILES[of_last] else (pool_add, POOL_ADDS)
                        n = adds_until(old, of_last) - (0 if kt >= PBUF else adds[False])
                        act.wait_ge(adder, adds_before(adds, pair, qb) + n)
                    nc.scalar.activation(prob[:, kt % PBUF], g.ps_s[:, kt % 2].rearrange("p h n -> p (h n)"),
                                         ACT.Exp, scale=g.exp_scale[:]).then_inc(exp_done, 1)
                    if kt == 0 and not first:
                        copy_output(it)
                if last:
                    copy_output(it + 1)

            def copy_output(blocks):
                act.wait_ge(g.pv_done, 1 + blocks * KT)
                act.wait_ge(norm_done, blocks * NP)
                nc.scalar.activation(o_raw[:], g.ps_o, ACT.Copy).then_inc(o_copied, 1)

            act.sem_inc(o_copied, 1)
            act.sem_inc(y_ready, 4)
            with act.Fori(0, B) as b:
                with act.Fori(0, 2) as hp:
                    it0 = (b * 2 + hp) * NB
                    for j, gn in enumerate((g.gn_a, g.gn_b)):
                        nc.scalar.activation(pair_gn[:, j], gn[:, bass.ds(b * CB, CB)], ACT.Copy)
                    for j in range(2):
                        last = nc.scalar.activation(pair_bias[:, j:j + 1], g.qk_bias[:, bass.ds(hp + 2 * j, 1)], ACT.Copy)
                    last.then_inc(bias_ready, 1)
                    act.wait_ge(bias_ready, b * 2 + hp + 1)
                    for s in range(2):
                        act.wait_ge(g.xn_in[s], 16 * (b * 2 + hp + 1))
                        for c in range(CB):
                            nc.scalar.activation(xn[:, s, c], xn[:, s, c], ACT.Identity, bias=pair_gn[:, 1, c:c + 1],
                                                 scale=pair_gn[:, 0, c:c + 1]).then_inc(xn_ready, 1)
                    act.wait_ge(g.pv_done, 1 + it0 * KT)
                    with act.Fori(0, NB // 2) as n2:
                        for s in range(2):
                            project(b, hp, n2, s)
                    softmax(b * 2 + hp, 0, True)
                    with act.Fori(1, NB - 1) as qb:
                        softmax(b * 2 + hp, qb, False)
                    softmax(b * 2 + hp, NB - 1, False, True)
                sign_weights(nc, act, g, g.signs0, 0, b)

        @block.tensor
        def _(pe):
            mm = nc.tensor.matmul

            def project(b, hp, n2, s, maxima):
                it0 = (b * 2 + hp) * NB
                pn = it0 + n2 * 2 + s
                pe.wait_ge(g.w_staged, 16 * (b * 2 + hp + 1))
                pe.wait_ge(xn_ready, (pn + 1) * CB)
                pe.wait_ge(y_ready, 2 + pn * 2)
                if not maxima:
                    pe.wait_ge(x1_ready, (b * NB + 1 + s) * CB)
                for j in range(2):
                    for c in range(CB):
                        ins = mm(g.ps_s[:, s, j], wst[:, c, j, :], xn[:, s, c, :], start=(c == 0), stop=(c == CB - 1))
                        if c == CB - 1:
                            ins.then_inc(g.proj_ready, 1)
                        if maxima:
                            first_maxima(it0, n2 - 1, s, [2 * j + c])
                pe.wait_ge(v_copied, 1 + pn)
                if not maxima:
                    pe.wait_ge(norm_done if s else o_copied, it0 * NP + NP if s else it0 + 1)
                for t in range(QT):
                    for c in range(CB):
                        last = mm(ps_v[s][:, t * P:(t + 1) * P], xn[:, s, c, t * P:(t + 1) * P], wst[:, c, 2, :],
                                  start=(c == 0), stop=(c == CB - 1))
                    if maxima and t == 1:
                        first_maxima(it0, n2 - 1, s, [4, 5])
                last.then_inc(g.proj_ready, 1)
                if maxima:
                    first_maxima(it0, n2 - 1, s, [6, 7])

            def first_maxima(it, n2, s, units):
                if units[0] == 0:
                    pe.wait_ge(qhi_copied, 2 * (it + n2 * 2 + s + 1))
                    pe.wait_ge(klo_done, 2 * (it + n2 * 2 + s + 3))
                for n in units:
                    h, t = n // QT, n % QT
                    pe.wait_ge(mx_used, 1 + it * UNITS + (n2 * 2 + s) * (2 * QT) + n)
                    mm(g.ps_max[:, n % 2], q1[h][:, t * P:(t + 1) * P], k1[h][:, cols(n2 * 2 + s)],
                       start=True, stop=True).then_inc(mx_ready, 1)

            def next_maxima(it, qb, units):
                for u in units:
                    h, t, kb = u // (QT * NB), u // NB % QT, u % NB
                    pe.wait_ge(mx_used, 1 + it * UNITS + u)
                    mm(g.ps_max[:, u % 2], q1[h][:, bass.ds(qb * TB + t * P, P)], k1[h][:, kb * TB:(kb + 1) * TB],
                       start=True, stop=True).then_inc(mx_ready, 1)

            def max_rows(it):
                pe.wait_ge(m_neg_ready, it + 1)
                for h in range(2):
                    last = mm(g.ps_misc[0:QT, h * P:(h + 1) * P], m_neg[:, h * QT:(h + 1) * QT], ident,
                              start=True, stop=True)
                last.then_inc(m_rows, 1)

            def column_sums(pair, qb, last):
                if last:
                    pe.wait_ge(pool_add, adds_before(POOL_ADDS, pair, qb) + POOL_ADDS[True])
                    pe.wait_ge(dve_add, adds_before(DVE_ADDS, pair, qb) + DVE_ADDS[True])
                else:
                    pe.wait_ge(tot_ready, pair * (NB - 1) + qb + 2)
                parts = [acc_pool, acc_dve] if last else [tot]
                for part in parts:
                    for h in range(2):
                        ins = mm(g.ps_misc[own[h], :], g.ones[:, 0:HD], part[:, h * TB:(h + 1) * TB],
                                 start=(part is parts[0]), stop=(part is parts[-1]))
                ins.then_inc(sum_ready, 1)

            def values(tiles, kt):
                pe.wait_ge(exp_done, tiles)
                for h in range(2):
                    last = mm(g.ps_o[own[h], :], vals[:, kt, own[h]], prob[:, kt % PBUF, h * TB:(h + 1) * TB],
                              start=(kt == 0), stop=(kt == KT - 1))
                last.then_inc(g.pv_done, 1)

            def query_block(it, pair, qb, first, with_max):
                for kt in range(KT):
                    if kt >= 2 or not first:
                        pe.wait_ge(exp_done, it * KT + (kt - 1))
                    keys = slice(kt * P, (kt + 1) * P)
                    for h in range(2):
                        if h and with_max:
                            next_maxima(it + 1, qb + 1, units_of(kt)[0])
                        mm(g.ps_s[:, kt % 2, h], k1[h][:, keys], q1[h][:, cols(qb)], start=True, stop=False)
                        if kt == 0:
                            pe.wait_ge(q2_ready, it * 2 + (h + 1))
                        last = mm(g.ps_s[:, kt % 2, h], k2[h][:, keys], q2[h][:, cols(qb)], start=False, stop=True)
                    last.then_inc(s_ready, 1)
                    if with_max:
                        next_maxima(it + 1, qb + 1, units_of(kt)[1])
                    if kt == 1 and not first:
                        pe.wait_ge(o_copied, it + 1)
                    if kt or not first:
                        values(it * KT + kt, (kt - 1) % KT)
                    if with_max:
                        next_maxima(it + 1, qb + 1, units_of(kt)[2])
                    if kt == 5 and not first:
                        column_sums(pair, qb - 1, False)
                    if kt == ROWS_AT and with_max:
                        if not first:
                            pe.wait_ge(norm_done, it * NP + NP)
                        max_rows(it + 1)
                if not with_max:
                    values(it * KT + KT, KT - 1)

            def output_projection(b, n2, s, later):
                pe.wait_ge(norm_done, b * (2 * NB * NP) + (2 * NB - later + 1) * NP)
                pe.wait_ge(x1_ready, (b * NB + n2 * 2 + s + 1) * CB)
                for m in range(CB):
                    for c in range(CB):
                        last = mm(g.ps_s[:, s, m], g.proj_w[:, c, m * P:(m + 1) * P],
                                  o_all[:, c, cols(n2 * 2 + s)], start=(c == 0), stop=(c == CB - 1))
                last.then_inc(out_ready, 1)

            with pe.Fori(0, B) as b:
                with pe.Fori(0, 2) as hp:
                    pair = b * 2 + hp
                    it0 = pair * NB
                    for s in range(2):
                        project(b, hp, 0, s, False)
                    with pe.Fori(1, NB // 2) as n2:
                        for s in range(2):
                            project(b, hp, n2, s, True)
                    for s in range(2):
                        first_maxima(it0, NB // 2 - 1, s, range(2 * QT))
                    pe.wait_ge(qlo_done, 4 + 2 * (it0 + NB))
                    pe.wait_ge(v_copied, 2 + it0 + NB)
                    max_rows(it0)
                    query_block(it0, pair, 0, True, True)
                    with pe.Fori(1, NB - 1) as qb:
                        query_block(it0 + qb, pair, qb, False, True)
                    query_block(it0 + (NB - 1), pair, NB - 1, False, False)
                    pe.wait_ge(norm_done, (it0 + NB) * NP)
                    column_sums(pair, NB - 1, True)
                with pe.Fori(0, NB // 2 - 1) as n2:
                    for s in range(2):
                        output_projection(b, n2, s, 1)
                output_projection(b, NB // 2 - 1, 0, 1)
                output_projection(b, NB // 2 - 1, 1, 0)

        @block.vector
        def _(dve):
            v = nc.vector
            dve.sem_inc(v_copied, 2)
            dve.sem_inc(norm_done, NP)
            dve.sem_inc(mx_used, 2)
            dve.sem_inc(x1_ready, 2 * CB)
            dve.sem_inc(x1_used, 2 * CB)
            for s in range(2):
                dve.sem_inc(g.y_out[s], 16)

            def split_q(b, hp, n2, s):
                pn = (b * 2 + hp) * NB + n2 * 2 + s
                here = cols(n2 * 2 + s)
                dve.wait_ge(g.pv_done, 1 + (b * 2 + hp) * (NB * KT))
                dve.wait_ge(hi_ready, pn * 2 + 1)
                for h in range(2):
                    v.tensor_copy(q1[h][other[h], here], q1[h][own[h], here]).then_inc(qhi_copied, 1)

            def copy_v(b, hp, n2, s):
                pn = (b * 2 + hp) * NB + n2 * 2 + s
                dve.wait_ge(g.proj_ready, 4 + (pn + 1) * 3)
                v.tensor_copy(vals[:, bass.ds((n2 * 2 + s) * QT, QT), :],
                              ps_v[s].rearrange("p (t d) -> p t d", t=QT)).then_inc(v_copied, 1)

            def first_maxima(it, n2, s, units):
                for n in units:
                    dve.wait_ge(mx_ready, it * UNITS + (n2 * 2 + s) * (2 * QT) + (n + 1))
                    v.tensor_reduce(m_part[:, bass.ds(n2 * 2 + (n * NB + s), 1)], g.ps_max[:, n % 2], AX.X,
                                    ALU.max).then_inc(mx_used, 1)

            def project_step(b, hp, n2, s):
                it0 = (b * 2 + hp) * NB
                before = (n2 - 1 + s, 1 - s)
                first_maxima(it0, n2 - 1, s, [0])
                copy_v(b, hp, *before)
                first_maxima(it0, n2 - 1, s, [1])
                split_q(b, hp, *before)
                first_maxima(it0, n2 - 1, s, [2])
                first_maxima(it0, n2 - 1, s, [3, 4, 5, 6, 7])

            def next_maxima(it, units):
                for u in units:
                    dve.wait_ge(mx_ready, it * UNITS + (u + 1))
                    v.tensor_reduce(m_part[:, u:u + 1], g.ps_max[:, u % 2], AX.X, ALU.max).then_inc(mx_used, 1)

            def negate_max(it):
                dve.wait_ge(mx_used, 2 + it * UNITS + UNITS)
                v.tensor_reduce(m_max[:], m_part[:].rearrange("p (t k) -> p t k", k=NB), AX.X,
                                ALU.max).then_inc(m_max_done, 1)
                dve.wait_ge(m_max_done, it + 1)
                v.tensor_scalar(m_neg[:], m_max[:], -1.0 / SHIFT, None, ALU.mult).then_inc(m_neg_ready, 1)

            def write_max_rows(it, qb):
                dve.wait_ge(m_rows, it + 1)
                for h in range(2):
                    s0 = other[h].start
                    v.tensor_tensor(q2[h][s0:s0 + QT, cols(qb)].rearrange("p (a n) -> p a n", a=QT),
                                    g.ps_misc[0:QT, h * P:(h + 1) * P].unsqueeze(1).to_broadcast([QT, QT, P]),
                                    mask, ALU.mult).then_inc(q2_ready, 1)

            def normalize(it, hp, qb, part, parts):
                size = TB // parts
                c = slice(part * size, (part + 1) * size)
                if part == 0:
                    dve.wait_ge(sum_ready, it + 2)
                    dve.wait_ge(o_copied, it + 2)
                v.reciprocal(rec[:, c], g.ps_misc[:, c]).then_inc(rec_done, NP // parts)
                dve.wait_ge(rec_done, it * NP + (part + 1) * (NP // parts))
                v.tensor_tensor(o_all[:, bass.ds(hp, 1), bass.ds(qb * TB + part * size, size)].rearrange(
                    "p a n -> p (a n)"), o_raw[:, c], rec[:, c], ALU.mult).then_inc(norm_done, NP // parts)

            def query_block(it, pair, hp, qb, first, with_max):
                adds, tiles, base = 0, DVE_TILES[not with_max], adds_before(DVE_ADDS, pair, qb)
                for kt in range(KT + 1):
                    if with_max and kt < KT:
                        for units in units_of(kt):
                            next_maxima(it + 1, units)
                    if kt - 1 in tiles:
                        dve.wait_ge(exp_done, it * KT + kt)
                        tile = prob[:, (kt - 1) % PBUF]
                        if adds:
                            dve.wait_ge(dve_add, base + adds)
                            v.tensor_tensor(acc_dve[:], acc_dve[:], tile, ALU.add).then_inc(dve_add, 1)
                        else:
                            dve.wait_ge(sum_ready if first else tot_ready,
                                        it + 1 if first else pair * (NB - 1) + qb + 1)
                            v.tensor_copy(acc_dve[:], tile).then_inc(dve_add, 1)
                        adds += 1
                    if kt in NORM_PARTS and not first:
                        normalize(it - 1, hp, qb - 1, NORM_PARTS[kt], NP)
                    if kt == LAST_UNIT and with_max:
                        negate_max(it + 1)
                    if kt == ROWS_AT and with_max:
                        write_max_rows(it + 1, qb + 1)

            def residual(b, n2, s):
                nn = b * NB + n2 * 2 + s
                dve.wait_ge(out_ready, nn + 1)
                dve.wait_ge(g.x_in[s], b * (8 * PER_BATCH) + 16 * (NB - 2) + (n2 + 1) * 16)
                dve.wait_ge(g.y_out[s], 16 * (b * (NB // 2) + n2 + 1))
                dve.wait_ge(x1_used, (nn + 1) * CB)
                for m in range(CB):
                    v.scalar_tensor_tensor(out=x1t[:, s, m], in0=g.ps_s[:, s, m],
                                           scalar=g.proj_bias[:, m:m + 1], in1=xt[:, s, m],
                                           op0=ALU.add, op1=ALU.add).then_inc(x1_ready, 1)
                dve.wait_ge(x1_ready, (nn + 3) * CB)
                dve.sem_inc(g.x_used, 1)

            def statistics(b, n2, s):
                nn = b * NB + n2 * 2 + s
                for m in range(CB):
                    v.bn_stats(g.bn_st[:, m, bass.ds(nn, 1), :].rearrange("p a s -> p (a s)"),
                               x1t[:, s, m]).then_inc(x1_used, 1)

            with dve.Fori(0, B) as b:
                with dve.Fori(0, 2) as hp:
                    pair = b * 2 + hp
                    it0 = pair * NB
                    split_q(b, hp, 0, 0)
                    copy_v(b, hp, 0, 0)
                    with dve.Fori(1, NB // 2) as n2:
                        for s in range(2):
                            project_step(b, hp, n2, s)
                    split_q(b, hp, NB // 2 - 1, 1)
                    copy_v(b, hp, NB // 2 - 1, 1)
                    for s in range(2):
                        first_maxima(it0, NB // 2 - 1, s, range(2 * QT))
                    negate_max(it0)
                    write_max_rows(it0, 0)
                    query_block(it0, pair, hp, 0, True, True)
                    with dve.Fori(1, NB - 1) as qb:
                        query_block(it0 + qb, pair, hp, qb, False, True)
                    query_block(it0 + (NB - 1), pair, hp, NB - 1, False, False)
                    normalize(it0 + (NB - 1), hp, NB - 1, 0, 1)
                with dve.Fori(0, NB // 2) as n2:
                    for s in range(2):
                        residual(b, n2, s)
                        statistics(b, n2, s)


def convolutions(nc, x1_d, w1_t, out, g):
    with ExitStack() as ctx:
        def sem(name):
            return ctx.enter_context(nc.semaphore(name))

        def sb(name, shape, dt=F32):
            return ctx.enter_context(nc.sbuf_tensor(name, shape, dt))

        rows = sb("rows", [P, 2, CB, CR + 2, W])
        comb = sb("comb", [P, CB, 4, CR // 2, W])
        parts = sb("parts", [P, 2, CB, 2, 4, CR // 2, PW], F16)
        hid = sb("hid", [P, CB, B, N])
        signs1 = sb("signs1", [P, CB, TAPS, C], F16)
        wmid = sb("wmid", [P, 2, CB, 2, 3, C], F16)
        half1 = sb("half1", [P, CB, TB])
        mid = sb("mid", [P, CB, 2, TB])
        cs = sb("cs", [P, 2, 4])
        wmean = sb("wmean", [P, 1])
        bmv = sb("bmv", [P, CB, 2])
        bvar = sb("bvar", [P, CB])
        bstd = sb("bstd", [P, CB])
        brs = sb("brs", [P, CB])
        btmp = sb("btmp", [P, CB])
        bn_a = sb("bn_a", [P, 2, CB])
        bn_b = sb("bn_b", [P, 2, CB])
        signs = (g.signs0, signs1)
        res = [t[:].rearrange("p a c n -> p (a c n)").rearrange("p (m n) -> p m n", m=CB) for t in (g.xt, g.y_tile)]

        border = sem("border")
        small = sem("bn_small")
        bvar_ready, bstd_ready, bn_ready = sem("bvar_ready"), sem("bstd_ready"), sem("bn_ready")
        wsum_mm, scale_ready = sem("wsum_mm"), sem("scale_ready")
        wmid_step = sem("wmid_step")
        rows_in = [[sem(f"rows_in{s}{c}") for c in range(CB)] for s in range(2)]
        relu_done = sem("relu_done")
        zero_rows = sem("zero_rows")
        comb_done = sem("comb_done")
        hi_done, lo_done = sem("hi_done"), sem("lo_done")
        conv_ready = sem("conv_ready")
        half_done = sem("half_done")
        mid_done = sem("mid_done")
        conv_evac = sem("conv_evac")
        stats_done = sem("stats_done")
        res_in, res_out = [[sem(f"{name}{s}") for s in range(2)] for name in ("res_in", "res_out")]
        res_done = sem("res_done")
        block = ctx.enter_context(nc.Block())

        def where(k):
            b, q = k // BLOCKS % B, k % BLOCKS
            return b, q, max(q * CR - 1, 0), min((q + 1) * CR + 1, H)

        def slot_rows(k):
            b, q, first, end = where(k)
            return slice(first - (q * CR - 1), end - (q * CR - 1))

        @block.sync
        def _(sp):
            def load_rows(k):
                b, q, first, end = where(k)
                if k >= 2:
                    sp.wait_ge(comb_done, (k - 1) * CB * 4)
                for c in range(CB):
                    sp.dma_start(rows[:, k % 2, c, slot_rows(k), :].rearrange("p r w -> p (r w)"),
                                 x1_d[b, c, :, first * W:end * W]).then_inc(rows_in[k % 2][c], 16)

            def load_weights(c):
                sp.wait_ge(g.wsum_ready, CB + c)
                sp.dma_start(g.wf[:], w1_t[c]).then_inc(g.wf_in, 16)

            def load_residual(k):
                b, q, _, _ = where(k)
                sp.dma_start(res[k % 2], x1_d[b, :, :, q * CT:(q + 1) * CT].rearrange("c p n -> p c n")).then_inc(
                    res_in[k % 2], 16)

            for b in range(B):
                for s in range(2):
                    sp.wait_ge(g.y_out[s], 16 + 16 * (b + 1) * NB // 2)
                for q in range(BLOCKS):
                    load_rows(b * BLOCKS + q)
                    if q == 1:
                        load_weights(b)
            for k in range(2):
                load_residual(k)
            for k in range(B * BLOCKS):
                b, q, _, _ = where(k)
                sp.wait_ge(res_done, (k + 1) * CB)
                sp.dma_start(out[b, :, :, q * CT:(q + 1) * CT].rearrange("c p n -> p c n"), res[k % 2]).then_inc(
                    res_out[k % 2], 16)
                if k + 2 < B * BLOCKS:
                    sp.wait_ge(res_out[k % 2], 16 * (k // 2 + 1))
                    load_residual(k + 2)
            for s in range(2):
                sp.wait_ge(res_out[s], 16 * B * BLOCKS // 2)

        @block.gpsimd
        def _(pool):
            edges = parts[:].rearrange("p s c h k r w -> p (s c h k r) w")
            nc.gpsimd.memset(edges[:, :, 0:1], 0.0).then_inc(border, 1)
            nc.gpsimd.memset(edges[:, :, PW - 1:PW], 0.0).then_inc(border, 1)
            for l in range(2):
                for c in range(CB):
                    pool.wait_ge(g.sign_done, l * CB + c + 1)
                    g0, g1, g2 = (signs[l][:, c, 3 * i:3 * (i + 1), :] for i in range(3))
                    plus, minus = wmid[:, l, c, 0], wmid[:, l, c, 1]
                    base = (l * CB + c) * 3
                    nc.gpsimd.tensor_tensor(minus, g0, g2, ALU.add).then_inc(wmid_step, 1)
                    pool.wait_ge(wmid_step, base + 1)
                    nc.gpsimd.tensor_tensor(plus, minus, g1, ALU.add).then_inc(wmid_step, 1)
                    pool.wait_ge(wmid_step, base + 2)
                    nc.gpsimd.tensor_tensor(minus, minus, g1, ALU.subtract).then_inc(wmid_step, 1)
            for k in range(B * BLOCKS):
                b, q, _, _ = where(k)
                pool.wait_ge(res_in[k % 2], 16 * (k // 2 + 1))
                for m in range(CB):
                    pool.wait_ge(conv_evac, CB + (B * BLOCKS + k) * CB + m + 1)
                    nc.gpsimd.tensor_tensor(res[k % 2][:, m], res[k % 2][:, m], hid[:, m, b, q * CT:(q + 1) * CT],
                                            ALU.add).then_inc(res_done, 1)

        @block.scalar
        def _(act):
            def relu(l, k, blocks=range(CB)):
                b, q, first, end = where(k)
                dst = rows[:, k % 2, :, slot_rows(k), :]
                for c in blocks:
                    if l == 0:
                        act.wait_ge(rows_in[k % 2][c], 16 * (k // 2 + 1))
                    else:
                        act.wait_ge(comb_done, (k - 1) * CB * 4)
                    src = dst[:, c] if l == 0 else hid[:, c, b, first * W:end * W].rearrange("p (r w) -> p r w", w=W)
                    nc.scalar.activation(dst[:, c], src, ACT.Relu, bias=bn_b[:, l, c:c + 1],
                                         scale=bn_a[:, l, c:c + 1]).then_inc(relu_done, 1)

            def split_hi(k, blocks=range(CB)):
                if k >= 2:
                    act.wait_ge(conv_ready, (k - 1) * CB)
                for c in blocks:
                    for pos in range(4):
                        act.wait_ge(comb_done, (k * CB + c) * 4 + pos + 1)
                        nc.scalar.activation(parts[:, k % 2, c, 0, pos, :, 1:W + 1], comb[:, c, pos],
                                             ACT.Copy).then_inc(hi_done, 1)

            def half(l, k):
                for m in range(CB):
                    act.wait_ge(conv_ready, k * CB + m + 1)
                    act.wait_ge(mid_done, k * CB + m + 1)
                    nc.scalar.activation(half1[:, m], g.ps[:, 4 * m + 1, :], ACT.Copy,
                                         scale=cs[:, l, 1:2]).then_inc(half_done, 1)

            for l in range(2):
                act.wait_ge(bvar_ready, l + 1)
                nc.scalar.activation(bstd[:], bvar[:], ACT.Sqrt).then_inc(bstd_ready, 1)
                act.wait_ge(bn_ready, l + 1)
                k0, k1 = l * B * BLOCKS, (l + 1) * B * BLOCKS
                for c in range(CB):
                    relu(l, k0, [c])
                    split_hi(k0, [c])
                for k in range(k0, k1 + 1):
                    if k0 < k < k1:
                        split_hi(k)
                    if k + 1 < k1:
                        relu(l, k + 1)
                    if k == k0:
                        act.wait_ge(scale_ready, l + 1)
                    else:
                        half(l, k - 1)
                    if l == 0 and k % BLOCKS == 2:
                        sign_weights(nc, act, g, signs1, 1, k // BLOCKS)

        @block.tensor
        def _(pe):
            def weights(l, c, pos, dx):
                if pos in (1, 2):
                    return wmid[:, l, c, pos - 1, dx]
                return signs[l][:, c, (0 if pos == 0 else 6) + dx]

            def products(l, k2, s):
                k = k2 * 2 + s + l * B * BLOCKS
                for m in range(CB):
                    pe.wait_ge(conv_evac, k * CB + (m + 1))
                    if m:
                        pe.wait_ge(scale_ready, l + 1)
                    for c in range(CB):
                        pe.wait_ge(wmid_step, (l * CB + c + 1) * 3)
                        for pos in range(4):
                            pe.wait_ge(lo_done, k * (CB * 4) + (c * 4 + pos + 1))
                            for dx in range(3):
                                for h in range(2):
                                    last = nc.tensor.matmul(
                                        g.ps[:, 4 * m + pos, :], weights(l, c, pos, dx)[:, m * P:(m + 1) * P],
                                        parts[:, s, c, h, pos, :, dx:dx + W],
                                        start=(c + dx + h == 0), stop=(c == CB - 1 and dx == 2 and h == 1))
                    last.then_inc(conv_ready, 1)

            pe.sem_inc(conv_evac, CB)
            for l in range(2):
                pe.wait_ge(g.wsum_ready, (l + 1) * CB)
                pe.wait_ge(conv_evac, CB + l * B * BLOCKS * CB)
                for c in range(CB):
                    last = nc.tensor.matmul(g.ps[:, 7, 0:1], g.ones[:], g.wsum[:, l, c:c + 1],
                                            start=(c == 0), stop=(c == CB - 1))
                last.then_inc(wsum_mm, 1)
                if l == 0:
                    pe.wait_ge(border, 2)
                with pe.Fori(0, B * BLOCKS // 2) as k2:
                    for s in range(2):
                        products(l, k2, s)

        @block.vector
        def _(dve):
            v = nc.vector
            steps = [0]

            def step(ins):
                steps[0] += 1
                ins.then_inc(small, 1)
                dve.wait_ge(small, steps[0])

            def batch_norm(l):
                par, col = g.par, (BN0, BN1)[l]
                for m in range(CB):
                    step(v.bn_aggr(bmv[:, m, :], g.bn_st[:, m].rearrange("p n s -> p (n s)")))
                v.tensor_scalar(bvar[:], bmv[:, :, 1], BN_EPS, None, ALU.add).then_inc(bvar_ready, 1)
                dve.wait_ge(bstd_ready, l + 1)
                step(v.reciprocal(brs[:], bstd[:]))
                step(v.tensor_tensor(btmp[:], brs[:], par[:, col:col + 2], ALU.mult))
                step(v.tensor_scalar(bn_a[:, l, :], btmp[:], g.fscale[:, 2 + l:3 + l], None, ALU.mult))
                step(v.tensor_tensor(brs[:], bmv[:, :, 0], btmp[:], ALU.mult))
                step(v.tensor_tensor(btmp[:], par[:, col + 2:col + 4], brs[:], ALU.subtract))
                v.tensor_scalar(bn_b[:, l, :], btmp[:], g.fscale[:, 2 + l:3 + l], None, ALU.mult).then_inc(bn_ready, 1)

            def layer_scale(l):
                dve.wait_ge(wsum_mm, l + 1)
                step(v.tensor_scalar(wmean[:], g.ps[:, 7, 0:1], 1.0 / (C * C * TAPS * RANGE), None, ALU.mult))
                step(v.tensor_tensor(cs[:, l, 0:1], wmean[:], g.bound[:, 2 + l:3 + l], ALU.mult))
                for i, f in ((1, 0.5), (2, -0.5), (3, -1.0)):
                    last = v.tensor_scalar(cs[:, l, i:i + 1], cs[:, l, 0:1], f, None, ALU.mult)
                last.then_inc(scale_ready, 1)
                dve.wait_ge(scale_ready, l + 1)

            def lo_part(k, c, pos):
                dve.wait_ge(hi_done, (k * CB + c) * 4 + pos + 1)
                hi, lo = (parts[:, k % 2, c, h, pos, :, 1:W + 1] for h in range(2))
                v.tensor_tensor(lo, comb[:, c, pos], hi, ALU.subtract).then_inc(lo_done, 1)

            def combine(k):
                first = k % (B * BLOCKS) == 0
                b, q, _, _ = where(k)
                slot = rows[:, k % 2]
                edge = 0 if q == 0 else CR + 1 if q == BLOCKS - 1 else None
                if edge is not None:
                    if k >= 2:
                        dve.wait_ge(comb_done, (k - 1) * CB * 4)
                    v.memset(slot[:, :, edge, :], 0.0).then_inc(zero_rows, 1)
                    dve.wait_ge(zero_rows, 2 * (k // BLOCKS) + (1 if q == 0 else 2))
                for c in range(CB):
                    dve.wait_ge(relu_done, k * CB + c + 1)
                    if k:
                        dve.wait_ge(lo_done, ((k - 1) * CB + c + 1) * 4)
                    r = [slot[:, c, i:i + CR - 1:2, :] for i in range(4)]
                    for pos, (i, j, op) in enumerate(((0, 2, ALU.subtract), (1, 2, ALU.add), (2, 1, ALU.subtract),
                                                      (1, 3, ALU.subtract))):
                        v.tensor_tensor(comb[:, c, pos], r[i], r[j], op).then_inc(comb_done, 1)
                        if first and pos:
                            lo_part(k, c, pos - 1)
                    for pos in range(3 if first else 0, 4):
                        lo_part(k, c, pos)

            def evacuate(l, k):
                b, q, _, _ = where(k)
                for m in range(CB):
                    dve.wait_ge(half_done, k * CB + m + 1)
                    prod = g.ps[:, 4 * m:4 * m + 4, :].rearrange("p k (r w) -> p k r w", w=W)
                    dst = hid[:, m, b, q * CT:(q + 1) * CT].rearrange("p (r t w) -> p t r w", t=2, w=W)
                    for i in range(2):
                        last = v.scalar_tensor_tensor(out=mid[:, m, i], in0=g.ps[:, 4 * m + 2, :],
                                                      scalar=cs[:, l, 1 + i:2 + i], in1=half1[:, m],
                                                      op0=ALU.mult, op1=ALU.add)
                    last.then_inc(mid_done, 1)
                    dve.wait_ge(mid_done, (k + 1) * CB + m + 1)
                    for i in range(2):
                        last = v.scalar_tensor_tensor(out=dst[:, i], in0=prod[:, 3 * i],
                                                      scalar=cs[:, l, 3 * i:3 * i + 1],
                                                      in1=mid[:, m, i].rearrange("p (r w) -> p r w", w=W),
                                                      op0=ALU.mult, op1=ALU.add)
                    last.then_inc(conv_evac, 1)
                    dve.wait_ge(conv_evac, (k + 1) * CB + m + 1)
                    if l == 0:
                        for j in range(2):
                            n = q * 2 + j
                            v.bn_stats(g.bn_st[:, m, b * NB + n, :],
                                       hid[:, m, b, n * TB:(n + 1) * TB]).then_inc(stats_done, 1)

            dve.sem_inc(mid_done, CB)
            for l in range(2):
                if l:
                    dve.wait_ge(stats_done, B * NB * CB)
                batch_norm(l)
                k0, k1 = l * B * BLOCKS, (l + 1) * B * BLOCKS
                for k in range(k0, k1 + 1):
                    if k < k1:
                        combine(k)
                    if k == k0:
                        layer_scale(l)
                    else:
                        evacuate(l, k - 1)


def constants():
    c = np.zeros((P, NCONST), np.float32)
    c[:, IDENT:IDENT + P] = np.eye(P)
    size = C // GROUPS
    c[:, GAVG:GAVG + P] = np.kron(np.eye(P // size), np.ones((size, size))) / size
    for t in range(QT):
        c[t, MASK + t * P:MASK + (t + 1) * P] = 1.0
    return c


def columns(*vectors):
    return np.ascontiguousarray(np.concatenate([np.asarray(v).reshape(-1, P) for v in vectors]).T)


def kernel(**inputs):
    import concourse.bacc as bacc
    from concourse.bass_utils import run_bass_kernel_spmd

    a = {k: np.asarray(v) for k, v in inputs.items()}
    arrays = {
        "x": np.ascontiguousarray(a["x"].reshape(B, CB, P, N)),
        "qkv_t": np.ascontiguousarray(
            a["L0_conv_qkv_weight"].reshape(3, 2, P, CB, P).transpose(1, 4, 3, 0, 2).reshape(2, P, CB * 3 * P)),
        "proj_t": np.ascontiguousarray(a["L0_conv_proj_weight"].T.reshape(CB, P, C)),
        "w0_t": np.ascontiguousarray(a["L1_conv_w0"].transpose(1, 2, 3, 0).reshape(CB, P, TAPS * C)),
        "w1_t": np.ascontiguousarray(a["L1_conv_w1"].transpose(1, 2, 3, 0).reshape(CB, P, TAPS * C)),
        "par": columns(a["L0_conv_gn_weight"], a["L0_conv_gn_bias"], a["L0_conv_qkv_bias"], a["L0_conv_proj_bias"],
                       a["L1_conv_gamma0"], a["L1_conv_beta0"], a["L1_conv_gamma1"], a["L1_conv_beta1"]),
        "const": constants(),
    }
    nc = bacc.Bacc("TRN2", target_bir_lowering=False, num_devices=1)
    args = [nc.dram_tensor(f"in_{k}", v.shape, F32, kind="ExternalInput").ap() for k, v in arrays.items()]
    args.append(nc.dram_tensor("out_y", (B, CB, P, N), F32, kind="ExternalOutput").ap())
    build(nc, *args)
    r = run_bass_kernel_spmd(nc, [{f"in_{k}": v for k, v in arrays.items()}], core_ids=[0])
    return r.results[0]["out_y"].reshape(B, C, H, W)
```
